# Optimizing a Trainium2 kernel written in Bass

```python
import numpy as np
import jax
import jax.numpy as jnp

def _softmax(x, axis=-1):
    return jax.nn.softmax(x, axis=axis)

def _gelu(x):
    return jax.nn.gelu(x, approximate=True)

def _silu(x):
    return jax.nn.silu(x)

def _sigmoid(x):
    return jax.nn.sigmoid(x)

def _layernorm(x, axis=-1, eps=1e-05):
    m = jnp.mean(x, axis=axis, keepdims=True)
    v = jnp.var(x, axis=axis, keepdims=True)
    return (x - m) / jnp.sqrt(v + eps)

def _scatter_add(tgt, idx, src, axis=0):
    return tgt.at[idx].add(src)

def _segment_sum(src, seg, n):
    return jax.ops.segment_sum(src, seg, n)
kernel_name = 'mk_cond_resid_d2_seqx_r4_6ac99e'

def setup_inputs(seed: int=0):
    np.random.seed(seed)
    _w = jnp.asarray

    def _rec_inputs():
        import jax
        import jax.numpy as jnp
        _rk = jax.random.key(seed)
        x = -0.000125 + 0.9999 * jax.random.normal(jax.random.fold_in(_rk, 1), (16, 256, 256), jnp.float32)
        _lenS = 256 - jax.random.randint(jax.random.fold_in(_rk, 7), (16,), 0, max(1, 256 // 4) + 1, jnp.int32)
        _lenS2 = 256 - jax.random.randint(jax.random.fold_in(_rk, 8), (16,), 0, max(1, 256 // 4) + 1, jnp.int32)
        cond_1024 = jax.random.uniform(jax.random.fold_in(_rk, 11), (16, 256), jnp.float32, 0.0, 0.999927)
        return (x, cond_1024)
    x, cond_1024 = _rec_inputs()

    def _L0_cond_setup():
        import jax, jax.numpy as jnp
        import numpy as np
        DT = 0.001
        key = jax.random.key(seed)
        k1, k2 = jax.random.split(key)
        inputs = jax.random.normal(k1, (16, 512, 256), dtype=jnp.float32)
        initial_state = jax.random.uniform(k2, (16, 256), dtype=jnp.float32)
        return {'inputs': inputs, 'initial_state': initial_state}
    _L0_cond_all = _L0_cond_setup()
    _L0_cond_in = {k: v for k, v in _L0_cond_all.items() if k in ()}
    del _L0_cond_all

    def _L1_cond_setup():
        import jax, jax.numpy as jnp
        import numpy as np
        D, HS, HE, E, K = (256, 512, 256, 8, 2)
        B, T = (4, 256)
        N_SHARED = 1
        key = jax.random.key(seed)
        ks = jax.random.split(key, 9)
        g = lambda k, shape, s: jax.random.normal(k, shape, jnp.float32) * s
        return {'x': g(ks[0], (B, T, D), 1.0), 't_emb': g(ks[1], (B, D), 1.0), 'router_W': g(ks[2], (2 * D, E), 0.01), 'router_bias': jnp.zeros((E,), jnp.float32), 'w1': g(ks[3], (D, HS), 0.02), 'w3': g(ks[4], (D, HS), 0.02), 'w2': g(ks[5], (HS, D), 0.02), 'W1e': g(ks[6], (E, D, HE), 0.02), 'W2e': g(ks[7], (E, HE, D), 0.02)}
    _L1_cond_all = _L1_cond_setup()
    _L1_cond_in = {k: v for k, v in _L1_cond_all.items() if k in ('router_W', 'router_bias', 'w1', 'w3', 'w2', 'W1e', 'W2e')}
    del _L1_cond_all
    return {'x': x, 'cond_1024': cond_1024, 'L1_cond_router_W': _L1_cond_in['router_W'], 'L1_cond_router_bias': _L1_cond_in['router_bias'], 'L1_cond_w1': _L1_cond_in['w1'], 'L1_cond_w3': _L1_cond_in['w3'], 'L1_cond_w2': _L1_cond_in['w2'], 'L1_cond_W1e': _L1_cond_in['W1e'], 'L1_cond_W2e': _L1_cond_in['W2e']}

def reference(x, cond_1024, L1_cond_router_W, L1_cond_router_bias, L1_cond_w1, L1_cond_w3, L1_cond_w2, L1_cond_W1e, L1_cond_W2e):
    import jax
    import jax.numpy as jnp

    def _L0_cond_ref(inputs, initial_state):
        import jax, jax.numpy as jnp
        import numpy as np
        DT = 0.001
        rates = jax.nn.relu(inputs) * DT
        c = initial_state[:, None, :] + jnp.cumsum(rates, axis=1)
        fl = jnp.floor(c)
        prev = jnp.concatenate([jnp.floor(initial_state)[:, None, :], fl[:, :-1, :]], axis=1)
        spikes = fl - prev
        return spikes / DT

    def _L1_cond_ref(x, t_emb, router_W, router_bias, w1, w3, w2, W1e, W2e):
        import jax, jax.numpy as jnp
        import numpy as np
        D, HS, HE, E, K = (256, 512, 256, 8, 2)
        B, T = (4, 256)
        N_SHARED = 1
        Bb, Tt, C = x.shape
        xf = x.reshape(-1, C)
        tf = jnp.broadcast_to(t_emb[:, None, :], (Bb, Tt, C)).reshape(-1, C)
        N = xf.shape[0]
        shared = jax.nn.silu(xf @ w1) * (xf @ w3) @ w2
        s = jax.nn.sigmoid((jnp.concatenate([xf, tf], axis=-1) @ router_W).astype(jnp.float32))
        sel_scores = s + router_bias
        _, topk_idx = jax.lax.top_k(sel_scores, K)
        s_sel = jnp.take_along_axis(s, topk_idx, axis=1)
        denom = s_sel.sum(axis=1, keepdims=True)
        gates = jnp.where(denom > 1e-09, s_sel / (denom + 1e-09), 1.0 / K).astype(x.dtype)
        combine = jnp.zeros((N, E), x.dtype).at[jnp.arange(N)[:, None], topk_idx].add(gates)
        h = jax.nn.gelu(jnp.einsum('nc,ech->enh', xf, W1e), approximate=False)
        y = jnp.einsum('enh,ehc->enc', h, W2e)
        routed = jnp.einsum('ne,enc->nc', combine, y)
        return ((shared + routed) / (N_SHARED + K)).reshape(Bb, Tt, C)
    x = x + _L0_cond_ref(x, cond_1024)
    x = x + _L1_cond_ref(x, cond_1024, L1_cond_router_W, L1_cond_router_bias, L1_cond_w1, L1_cond_w3, L1_cond_w2, L1_cond_W1e, L1_cond_W2e)
    return x

_drawn_inputs = setup_inputs


def setup_inputs(seed=0):
    import zlib

    import numpy as np

    out = dict(_drawn_inputs(seed))
    spreads = {'L1_cond_router_bias': (0.0, 0.646)}
    factors = {'L1_cond_router_W': 5.024, 'L1_cond_W1e': 4.891, 'L1_cond_W2e': 4.037}
    for name, (base, spread) in spreads.items():
        noise = np.random.default_rng([zlib.crc32(name.encode()), seed]).standard_normal(out[name].shape)
        drawn = base * np.exp(spread * noise) if base else spread * noise
        out[name] = jnp.asarray(drawn.astype(out[name].dtype))
    for name, factor in factors.items():
        out[name] = (out[name] * factor).astype(out[name].dtype)
    return out
```

```python
import concourse.bass as bass
from concourse import mybir
from contextlib import ExitStack


def build_spiking_moe(nc, x_t, cond_t, router_w, router_b, w_all, out_t, gates_dram):
    F32 = mybir.dt.float32
    F32R = mybir.dt.float32r
    I32 = mybir.dt.int32
    U32 = mybir.dt.uint32
    ALU = mybir.AluOpType
    ACT = mybir.ActivationFunctionType
    AX = mybir.AxisListType

    P = 128
    CC, _, N = x_t.shape
    T = 256
    NB = cond_t.shape[2]
    E = router_b.shape[0]
    GT = 512
    NG = N // GT
    BG = GT // T
    TT = GT // P
    SHARED = 4
    BLOCKS = SHARED + 2 * E
    CHUNK = 1024
    UP_S, DN_S, PAIRS = 0, 2 * CHUNK, 3 * CHUNK
    NCHUNK = w_all.shape[1] // CHUNK
    DT = 0.001
    PER_SPIKE = 999.99993896484375
    THIRD = 1.0 / 3.0
    HRING, RING = 4, 3

    def up_cols(b, half, c):
        if b < SHARED:
            return UP_S + ((b * 2 + half) * CC + c) * P
        e, m = divmod(b - SHARED, 2)
        return PAIRS + (e // 2) * 2 * CHUNK + (((e % 2) * 2 + m) * CC + c) * P

    def dn_cols(b):
        if b < SHARED:
            return DN_S + b * CC * P
        e, m = divmod(b - SHARED, 2)
        return PAIRS + (e // 2) * 2 * CHUNK + CHUNK + ((e % 2) * 2 + m) * CC * P

    def chunk_of(col):
        return col // CHUNK

    ctx = ExitStack()
    with ctx:
        def sb(name, shape, dt=F32):
            return ctx.enter_context(nc.sbuf_tensor(name, shape, dt))

        def sem(name):
            return ctx.enter_context(nc.semaphore(name))

        w_hi = sb("w_hi", [P, NCHUNK * CHUNK], F32R)
        w_lo = sb("w_lo", [P, NCHUNK * CHUNK], F32R)
        NRAW = 3
        w_raw = sb("w_raw", [P, NRAW, CHUNK])
        rw = sb("rw", [P, 2 * CC, E])
        rb = sb("rb", [P, TT * E])
        cond = sb("cond", [P, CC, NB])
        cond_rw = sb("cond_rw", [P, CC, NB, E])
        cond_logit = sb("cond_logit", [P, NB, E])
        ones = sb("ones", [P, T])
        ident = sb("ident", [P, P])
        lane_e = sb("lane_e", [P, E])
        x_in = sb("x_in", [P, CC, BG, T])
        init = sb("init", [P, CC, BG])
        rates = sb("rates", [P, CC, BG, T])
        sums = sb("sums", [P, CC, BG, T])
        pot = sb("pot", [P, CC, BG, T + 1])
        pot_int = sb("pot_int", [P, CC, BG, T + 1], I32)
        above = sb("above", [P, CC, BG, T + 1])
        floors = sb("floors", [P, CC, BG, T + 1])
        x1 = sb("x1", [P, CC, GT])
        x1_keep = sb("x1_keep", [P, CC, GT])
        x_hi = sb("x_hi", [P, CC, GT], F32R)
        x_lo = sb("x_lo", [P, CC, GT], F32R)
        logit = sb("logit", [P, TT, E])
        score = sb("score", [P, TT, E])
        sel = sb("sel", [P, TT, E])
        top = sb("top", [P, TT, 8])
        top_i = sb("top_i", [P, TT, 8], U32)
        top_f = sb("top_f", [P, TT, 2])
        hot0 = sb("hot0", [P, TT, E])
        hot1 = sb("hot1", [P, TT, E])
        picked = sb("picked", [P, TT, E])
        denom = sb("denom", [P, TT])
        denom_e = sb("denom_e", [P, TT])
        recip = sb("recip", [P, TT])
        big = sb("big", [P, TT])
        half = sb("half", [P, TT])
        recip_g = sb("recip_g", [P, TT])
        combine = sb("combine", [P, TT, E])
        gate_t = sb("gate_t", [E, GT])
        gate_all = sb("gate_all", [P, E, GT])
        act = sb("act", [P, 2, GT])
        silu = sb("silu", [P, 2, GT])
        hid = sb("hid", [P, 2, GT])
        hid_hi = sb("hid_hi", [P, RING, GT], F32R)
        hid_lo = sb("hid_lo", [P, RING, GT], F32R)
        y_out = sb("y_out", [P, CC, GT])

        ps_h = [ctx.enter_context(nc.psum_tensor(f"ps_h{n}", [P, GT], F32)) for n in range(HRING)]
        ps_y = [ctx.enter_context(nc.psum_tensor(f"ps_y{n}", [P, GT], F32)) for n in range(CC)]
        ps_r = ctx.enter_context(nc.psum_tensor("ps_r", [P, GT], F32))
        ps_g = ctx.enter_context(nc.psum_tensor("ps_g", [P, GT], F32))

        s_w = [sem(f"w_loaded{n}") for n in range(NCHUNK)]
        s_small = sem("small_loaded")
        s_const = sem("const_made")
        s_whi = sem("w_hi_made")
        s_wlo = sem("w_lo_made")
        s_pw = sem("pool_w_hi_made")
        s_plo = sem("pool_w_lo_made")
        s_crw = sem("cond_rw_made")
        s_cl = sem("cond_logit_summed")
        s_clc = sem("cond_logit_kept")
        s_x = sem("x_loaded")
        s_front = sem("front_step")
        s_split_hi = sem("x_hi_made")
        s_split_lo = sem("x_lo_made")
        s_keep = sem("x1_kept")
        s_logit = sem("logits_summed")
        s_score = sem("scores_made")
        s_route = sem("route_step")
        s_gt = sem("gates_transposed")
        s_gc = sem("gates_copied")
        s_gs = sem("gates_stored")
        s_g = [sem(f"gates_spread{q}") for q in range(4)]
        s_held = sem("dve_held")
        s_sp_held = sem("sp_held")
        s_rg = sem("gate_terms")
        s_floor = sem("floors_made")
        s_spike = sem("spikes_made")
        s_up = sem("up_done")
        s_act = sem("act_done")
        s_silu = sem("silu_made")
        s_hid = sem("hidden_made")
        s_hhi = sem("hid_hi_made")
        s_hlo = sem("hid_lo_made")
        s_down = sem("down_done")
        s_fin = sem("y_made")
        s_out = sem("y_stored")

        FRONT_STEPS = 13
        ROUTE_STEPS = 22
        DVE_CHUNKS = 3

        block = ctx.enter_context(nc.Block())

        def after(engine, semaphore, count):
            if not (isinstance(count, int) and count == 0):
                engine.wait_ge(semaphore, count)

        @block.sync
        def _(sp):
            def load_x(j):
                sp.dma_start(x_in[:, :, :, :].rearrange("p c b t -> p c (b t)"),
                             x_t[:, :, bass.ds(j * GT, GT)].rearrange("c p n -> p c n")).then_inc(s_x, 16)
                sp.dma_start(init[:, :, :],
                             cond_t[:, :, bass.ds(j * BG, BG)]).then_inc(s_x, 16)

            def spread_gates(i):
                sp.wait_ge(s_gc, i + 1)
                sp.sem_inc(s_sp_held, 1)
                sp.dma_start(gates_dram[i], gate_t[:, :]).then_inc(s_gs, 16)
                sp.wait_ge(s_gs, i * 16 + 16)
                sp.sem_inc(s_sp_held, 1)
                after(sp, s_hid, i * BLOCKS)
                for q in range(4):
                    e0 = q * E // 4
                    sp.dma_start(gate_all[:, e0:e0 + E // 4, :].rearrange("p e n -> p (e n)"),
                                 gates_dram[i, e0:e0 + E // 4, :].rearrange("e n -> (e n)")
                                 .partition_broadcast(P)).then_inc(s_g[q], 16)

            def group(i, more):
                spread_gates(i)
                if more:
                    sp.wait_ge(s_front, (i + 1) * FRONT_STEPS)
                    sp.sem_inc(s_sp_held, 1)
                    load_x(i + 1)
                sp.wait_ge(s_fin, CC * (i + 1))
                sp.sem_inc(s_sp_held, 1)
                sp.dma_start(out_t[:, :, bass.ds(i * GT, GT)].rearrange("c p n -> p c n"),
                             y_out[:, :, :]).then_inc(s_out, 16)

            load_x(0)
            sp.dma_start(cond[:, :, :], cond_t).then_inc(s_small, 16)
            sp.dma_start(rw[:, :, :], router_w).then_inc(s_small, 16)
            for t in range(TT):
                sp.dma_start(rb[:, t * E:(t + 1) * E], router_b.partition_broadcast(P)).then_inc(s_small, 16)
            for k in range(NCHUNK):
                if k >= NRAW:
                    j = k - NRAW
                    sp.wait_ge(s_wlo if j < DVE_CHUNKS else s_plo, (j if j < DVE_CHUNKS else j - DVE_CHUNKS) + 1)
                sp.dma_start(w_raw[:, k % NRAW, :], w_all[:, k * CHUNK:(k + 1) * CHUNK]).then_inc(s_w[k], 16)
            group(0, True)
            with nc.sync.Fori(1, NG - 1) as i:
                group(i, True)
            group(NG - 1, False)
            sp.wait_ge(s_out, NG * 16)

        @block.gpsimd
        def _(pool):
            nc.gpsimd.memset(ones[:, :], 1.0).then_inc(s_const, 1)
            nc.gpsimd.memset(ident[:, :], 0.0).then_inc(s_const, 1)
            nc.gpsimd.iota(lane_e[:, :], pattern=[[1, E]], base=0, channel_multiplier=0,
                           allow_small_or_imprecise_dtypes=True).then_inc(s_const, 1)
            pool.wait_ge(s_const, 2)
            nc.gpsimd.affine_select(out=ident[:, :], in_=ident[:, :], compare_op=ALU.not_equal, fill=1.0,
                                    base=0, pattern=[[-1, P]], channel_multiplier=1).then_inc(s_const, 1)
            for k in range(DVE_CHUNKS, NCHUNK):
                cols = slice(k * CHUNK, (k + 1) * CHUNK)
                pool.wait_ge(s_w[k], 16)
                nc.gpsimd.tensor_copy(w_hi[:, cols], w_raw[:, k % NRAW, :]).then_inc(s_pw, 1)
                pool.wait_ge(s_pw, k - DVE_CHUNKS + 1)
                nc.gpsimd.tensor_tensor(w_lo[:, cols], w_raw[:, k % NRAW, :], w_hi[:, cols].bitcast(F32),
                                        ALU.subtract).then_inc(s_plo, 1)

            def keep(i):
                pool.wait_ge(s_split_lo, i + 1)
                after(pool, s_fin, CC * i)
                nc.gpsimd.tensor_tensor(x1_keep[:, :, :], x_hi[:, :, :].bitcast(F32), x_lo[:, :, :].bitcast(F32),
                                        ALU.add).then_inc(s_keep, 1)

            keep(0)
            with nc.gpsimd.Fori(1, NG) as i:
                keep(i)

        @block.scalar
        def _(act_e):
            def group(i):
                act_e.wait_ge(s_front, (i + 1) * FRONT_STEPS)
                after(act_e, s_up, i * BLOCKS)
                after(act_e, s_keep, i)
                nc.scalar.activation(x_hi[:, :, :], x1[:, :, :], ACT.Copy).then_inc(s_split_hi, 1)
                act_e.wait_ge(s_route, i * ROUTE_STEPS + 1)
                nc.scalar.activation(score[:, :, :], logit[:, :, :], ACT.Sigmoid).then_inc(s_score, 1)
                for b in range(BLOCKS):
                    act_e.wait_ge(s_up, i * BLOCKS + b + 1)
                    after(act_e, s_hid, i * BLOCKS + max(b - 1, 0))
                    bank = 2 * b if b < SHARED else b + SHARED
                    nc.scalar.activation(act[:, b % 2, :], ps_h[bank % HRING][:, :],
                                         ACT.Sigmoid if b < SHARED else ACT.Gelu).then_inc(s_act, 1)
                    if b == 1:
                        act_e.wait_ge(s_gt, i + 1)
                        after(act_e, s_gs, i * 16)
                        nc.scalar.activation(gate_t[:, :], ps_g[0:E, :], ACT.Copy).then_inc(s_gc, 1)
                    act_e.wait_ge(s_hid, i * BLOCKS + b + 1)
                    after(act_e, s_down, i * BLOCKS + max(b - RING + 1, 0))
                    nc.scalar.activation(hid_hi[:, b % RING, :], hid[:, b % 2, :], ACT.Copy).then_inc(s_hhi, 1)

            for k in range(DVE_CHUNKS):
                act_e.wait_ge(s_w[k], 16)
                nc.scalar.activation(w_hi[:, k * CHUNK:(k + 1) * CHUNK], w_raw[:, k % NRAW, :],
                                     ACT.Copy).then_inc(s_whi, 1)
            act_e.wait_ge(s_cl, 1)
            nc.scalar.activation(cond_logit[:, :, :].rearrange("p b e -> p (b e)"), ps_r[:, 0:NB * E],
                                 ACT.Copy).then_inc(s_clc, 1)
            group(0)
            with nc.scalar.Fori(1, NG) as i:
                group(i)

        @block.vector
        def _(dve):
            x_flat = x_in[:, :, :, :].rearrange("p c b t -> p (c b t)")

            def front_steps(j):
                n = [0]

                def done(ins):
                    n[0] += 1
                    ins.then_inc(s_front, 1)

                def need(k):
                    dve.wait_ge(s_front, j * FRONT_STEPS + k)

                def rate():
                    dve.wait_ge(s_x, j * 32 + 32)
                    done(nc.vector.tensor_scalar(rates[:, :, :, :].rearrange("p c b t -> p (c b t)"), x_flat,
                                                 0.0, DT, ALU.max, ALU.mult))

                def start_col():
                    done(nc.vector.tensor_copy(pot[:, :, :, 0], init[:, :, :]))

                def scan(q):
                    c, b = divmod(q, BG)
                    if q == 0:
                        need(1)
                    done(nc.vector.tensor_tensor_scan(sums[:, c, b, :], ones[:, :], rates[:, c, b, :], 0.0,
                                                      ALU.mult, ALU.add))

                def add_init(q):
                    c, b = divmod(q, BG)
                    need(3 + q)
                    done(nc.vector.tensor_scalar(pot[:, c, b, 1:T + 1], sums[:, c, b, :], init[:, c, b:b + 1],
                                                 None, ALU.add))

                flat = lambda t: t[:, :, :, :].rearrange("p c b t -> p (c b t)")

                def to_int():
                    need(10)
                    done(nc.vector.tensor_copy(flat(pot_int), flat(pot)))

                def rounded_up():
                    need(11)
                    done(nc.vector.tensor_tensor(flat(above), flat(pot_int), flat(pot), ALU.is_gt))

                def floor():
                    need(12)
                    nc.vector.tensor_tensor(flat(floors), flat(pot_int), flat(above),
                                            ALU.subtract).then_inc(s_floor, 1)

                def spikes():
                    dve.wait_ge(s_floor, j + 1)
                    nc.vector.tensor_tensor(sums[:, :, :, :], floors[:, :, :, 1:T + 1], floors[:, :, :, 0:T],
                                            ALU.subtract).then_inc(s_spike, 1)

                def new_x1():
                    dve.wait_ge(s_spike, j + 1)
                    after(dve, s_split_hi, j)
                    after(dve, s_logit, j)
                    done(nc.vector.scalar_tensor_tensor(
                        x1[:, :, :].rearrange("p c n -> p (c n)"), sums[:, :, :, :].rearrange("p c b t -> p (c b t)"),
                        PER_SPIKE, x_flat, ALU.mult, ALU.add))

                return [rate, start_col, *[lambda q=q: scan(q) for q in range(4)],
                        *[lambda q=q: add_init(q) for q in range(4)], to_int, rounded_up, floor, spikes, new_x1]

            def route(i):
                n = [0]

                def done(ins):
                    n[0] += 1
                    ins.then_inc(s_route, 1)

                def need_last():
                    dve.wait_ge(s_route, i * ROUTE_STEPS + n[0])

                def spread(t):
                    return t[:, :].unsqueeze(2).to_broadcast([P, TT, E])

                dve.wait_ge(s_logit, i + 1)
                for b in range(BG):
                    r = slice(b * TT // BG, (b + 1) * TT // BG)
                    last = nc.vector.tensor_tensor(
                        logit[:, r, :], ps_r[:, b * TT // BG * E:(b + 1) * TT // BG * E].rearrange("p (t e) -> p t e", e=E),
                        cond_logit[:, bass.ds(i * BG + b, 1), :].to_broadcast([P, TT // BG, E]), ALU.add)
                done(last)
                dve.wait_ge(s_score, i + 1)
                done(nc.vector.tensor_tensor(sel[:, :, :].rearrange("p t e -> p (t e)"),
                                             score[:, :, :].rearrange("p t e -> p (t e)"), rb[:, :], ALU.add))
                need_last()
                dve.sem_inc(s_held, 1)
                for t in range(TT):
                    done(nc.vector.max(top[:, t, :], sel[:, t, :]))
                need_last()
                dve.sem_inc(s_held, 1)
                for t in range(TT):
                    done(nc.vector.max_index(top_i[:, t, :], top[:, t, :], sel[:, t, :]))
                need_last()
                done(nc.vector.tensor_copy(top_f[:, :, :], top_i[:, :, 0:2]))
                need_last()
                for k, hot in enumerate((hot0, hot1)):
                    done(nc.vector.tensor_tensor(hot[:, :, :], lane_e[:, :].unsqueeze(1).to_broadcast([P, TT, E]),
                                                 top_f[:, :, k:k + 1].to_broadcast([P, TT, E]), ALU.is_equal))
                need_last()
                done(nc.vector.tensor_tensor(hot0[:, :, :], hot0[:, :, :], hot1[:, :, :], ALU.add))
                need_last()
                done(nc.vector.tensor_tensor(picked[:, :, :], hot0[:, :, :], score[:, :, :], ALU.mult))
                need_last()
                done(nc.vector.tensor_reduce(denom[:, :], picked[:, :, :], axis=AX.X, op=ALU.add))
                need_last()
                done(nc.vector.tensor_scalar(denom_e[:, :], denom[:, :], 1e-9, None, ALU.add))
                done(nc.vector.tensor_scalar(big[:, :], denom[:, :], 1e-9, None, ALU.is_gt))
                need_last()
                done(nc.vector.reciprocal(recip[:, :], denom_e[:, :]))
                done(nc.vector.tensor_scalar(half[:, :], big[:, :], -0.5, 0.5, ALU.mult, ALU.add))
                need_last()
                done(nc.vector.tensor_tensor(recip_g[:, :], recip[:, :], big[:, :], ALU.mult))
                need_last()
                after(dve, s_gt, i)
                nc.vector.tensor_tensor(picked[:, :, :], picked[:, :, :], recip_g[:, :].unsqueeze(2).to_broadcast([P, TT, E]), ALU.mult).then_inc(s_rg, 1)
                nc.vector.tensor_tensor(hot1[:, :, :], hot0[:, :, :], half[:, :].unsqueeze(2).to_broadcast([P, TT, E]), ALU.mult).then_inc(s_rg, 1)
                dve.wait_ge(s_rg, i * 2 + 2)
                done(nc.vector.tensor_tensor(combine[:, :, :], picked[:, :, :], hot1[:, :, :], ALU.add))
                assert n[0] == ROUTE_STEPS, n[0]

            def split_x(i):
                dve.wait_ge(s_split_hi, i + 1)
                nc.vector.tensor_tensor(x_lo[:, :, :], x1[:, :, :], x_hi[:, :, :].bitcast(F32),
                                        ALU.subtract).then_inc(s_split_lo, 1)

            def finish(i):
                dve.wait_ge(s_down, (i + 1) * BLOCKS)
                dve.wait_ge(s_keep, i + 1)
                after(dve, s_out, i * 16)
                for c in range(CC):
                    nc.vector.scalar_tensor_tensor(y_out[:, c, :], ps_y[c][:, :], THIRD, x1_keep[:, c, :],
                                                   ALU.mult, ALU.add).then_inc(s_fin, 1)

            def group(i, more):
                split_x(i)
                route(i)
                steps = front_steps(i + 1) if more else []
                for b in range(BLOCKS):
                    n = i * BLOCKS + b
                    dve.wait_ge(s_act, n + 1)
                    after(dve, s_hhi, i * BLOCKS + max(b - 1, 0))
                    if b < SHARED:
                        nc.vector.tensor_tensor(silu[:, b % 2, :], act[:, b % 2, :], ps_h[2 * b % HRING][:, :],
                                                ALU.mult).then_inc(s_silu, 1)
                        dve.wait_ge(s_silu, i * SHARED + b + 1)
                        nc.vector.tensor_tensor(hid[:, b % 2, :], silu[:, b % 2, :], ps_h[(2 * b + 1) % HRING][:, :],
                                                ALU.mult).then_inc(s_hid, 1)
                    else:
                        e = (b - SHARED) // 2
                        if (b - SHARED) % 4 == 0:
                            dve.wait_ge(s_g[e // 2], i * 16 + 16)
                        nc.vector.tensor_tensor(hid[:, b % 2, :], act[:, b % 2, :], gate_all[:, e, :],
                                                ALU.mult).then_inc(s_hid, 1)
                        if steps:
                            steps.pop(0)()
                    dve.wait_ge(s_hhi, n + 1)
                    after(dve, s_down, i * BLOCKS + max(b - RING + 1, 0))
                    nc.vector.tensor_tensor(hid_lo[:, b % RING, :], hid[:, b % 2, :],
                                            hid_hi[:, b % RING, :].bitcast(F32), ALU.subtract).then_inc(s_hlo, 1)
                assert not steps
                finish(i)

            dve.wait_ge(s_small, 16 * (2 + TT))
            for c in range(CC):
                nc.vector.tensor_tensor(cond_rw[:, c, :, :], cond[:, c, :].unsqueeze(2).to_broadcast([P, NB, E]),
                                        rw[:, CC + c, :].unsqueeze(1).to_broadcast([P, NB, E]),
                                        ALU.mult).then_inc(s_crw, 1)
            dve.wait_ge(s_const, 4)
            for step in front_steps(0):
                step()
            for k in range(DVE_CHUNKS):
                dve.wait_ge(s_whi, k + 1)
                cols = slice(k * CHUNK, (k + 1) * CHUNK)
                nc.vector.tensor_tensor(w_lo[:, cols], w_raw[:, k % NRAW, :], w_hi[:, cols].bitcast(F32),
                                        ALU.subtract).then_inc(s_wlo, 1)
            dve.wait_ge(s_clc, 1)
            group(0, True)
            with nc.vector.Fori(1, NG - 1) as i:
                group(i, True)
            group(NG - 1, False)

        @block.tensor
        def _(pe):
            def ready(col):
                k = chunk_of(col)
                if k < DVE_CHUNKS:
                    pe.wait_ge(s_wlo, k + 1)
                else:
                    pe.wait_ge(s_plo, k - DVE_CHUNKS + 1)

            def three(out, w_col, hi, lo, start, stop):
                wh, wl = w_hi[:, w_col:w_col + P], w_lo[:, w_col:w_col + P]
                nc.tensor.matmul(out, wh, hi, start=start, stop=False)
                nc.tensor.matmul(out, wh, lo, start=False, stop=False)
                return nc.tensor.matmul(out, wl, hi, start=False, stop=stop)

            def up(i, b):
                ready(up_cols(b, 0, 0))
                if b in (2, 3):
                    pe.wait_ge(s_hid, i * BLOCKS + b - 1)
                elif SHARED <= b < 2 * SHARED:
                    pe.wait_ge(s_hid, i * BLOCKS + 2 + (b - SHARED) // 2 + 1)
                elif b >= 2 * SHARED:
                    pe.wait_ge(s_act, i * BLOCKS + b - HRING + 1)
                for half in range(2 if b < SHARED else 1):
                    bank = 2 * b + half if b < SHARED else b + SHARED
                    for c in range(CC):
                        last = three(ps_h[bank % HRING][:, :], up_cols(b, half, c), x_hi[:, c, :], x_lo[:, c, :],
                                     c == 0, c == CC - 1)
                last.then_inc(s_up, 1)

            def down(i, b):
                ready(dn_cols(b))
                pe.wait_ge(s_hhi, i * BLOCKS + b + 1)
                pe.wait_ge(s_hlo, i * BLOCKS + b + 1)
                if b == 0:
                    after(pe, s_fin, CC * i)
                for c in range(CC):
                    last = three(ps_y[c][:, :], dn_cols(b) + c * P, hid_hi[:, b % RING, :], hid_lo[:, b % RING, :],
                                 b == 0, b == BLOCKS - 1)
                last.then_inc(s_down, 1)

            def logits(i):
                pe.wait_ge(s_front, (i + 1) * FRONT_STEPS)
                after(pe, s_route, i * ROUTE_STEPS)
                for t in range(TT):
                    for c in range(CC):
                        last = nc.tensor.matmul(ps_r[:, t * E:(t + 1) * E], x1[:, c, t * P:(t + 1) * P], rw[:, c, :],
                                                start=(c == 0), stop=(c == CC - 1))
                last.then_inc(s_logit, 1)

            def gates(i):
                pe.wait_ge(s_route, (i + 1) * ROUTE_STEPS)
                after(pe, s_gc, i)
                for t in range(TT):
                    last = nc.tensor.transpose(ps_g[0:E, t * P:(t + 1) * P], combine[:, t, :], ident[:, :])
                last.then_inc(s_gt, 1)

            def group(i):
                logits(i)
                pe.wait_ge(s_split_hi, i + 1)
                pe.wait_ge(s_split_lo, i + 1)
                for b in range(BLOCKS):
                    up(i, b)
                    if b == 1:
                        gates(i)
                    if b >= 2:
                        down(i, b - 2)
                down(i, BLOCKS - 2)
                down(i, BLOCKS - 1)

            pe.wait_ge(s_const, 4)
            pe.wait_ge(s_small, 16 * (2 + TT))
            pe.wait_ge(s_crw, CC)
            for c in range(CC):
                last = nc.tensor.matmul(ps_r[:, 0:NB * E], ones[:, 0:P],
                                        cond_rw[:, c, :, :].rearrange("p b e -> p (b e)"),
                                        start=(c == 0), stop=(c == CC - 1))
            last.then_inc(s_cl, 1)
            pe.wait_ge(s_clc, 1)
            group(0)
            with nc.tensor.Fori(1, NG) as i:
                group(i)


def kernel(**inputs):
    import numpy as np
    import concourse.bacc as bacc
    from concourse.bass_utils import run_bass_kernel_spmd

    P = 128
    f = {k: np.asarray(v) for k, v in inputs.items()}
    x = f["x"]
    B, T, C = x.shape
    CC = C // P
    w1, w3, w2 = f["L1_cond_w1"], f["L1_cond_w3"], f["L1_cond_w2"]
    w1e, w2e = f["L1_cond_W1e"], f["L1_cond_W2e"]
    E = w1e.shape[0]

    def up_block(w):
        return w.reshape(CC, P, P).transpose(1, 0, 2).reshape(P, C)

    cols = []
    for b in range(w1.shape[1] // P):
        for w in (w1, w3):
            cols.append(up_block(w[:, b * P:(b + 1) * P]))
    for b in range(w2.shape[0] // P):
        cols.append(w2[b * P:(b + 1) * P, :])
    for e0 in range(0, E, 2):
        for e in (e0, e0 + 1):
            for m in range(w1e.shape[2] // P):
                cols.append(up_block(w1e[e][:, m * P:(m + 1) * P]))
        for e in (e0, e0 + 1):
            for m in range(w2e.shape[1] // P):
                cols.append(w2e[e][m * P:(m + 1) * P, :])
    arrays = {
        "x_t": np.ascontiguousarray(x.transpose(2, 0, 1).reshape(CC, P, B * T)),
        "cond_t": np.ascontiguousarray(f["cond_1024"].T.reshape(CC, P, B).transpose(1, 0, 2)),
        "router_w": np.ascontiguousarray(f["L1_cond_router_W"].reshape(2 * CC, P, E).transpose(1, 0, 2)),
        "router_b": np.ascontiguousarray(f["L1_cond_router_bias"]),
        "w_all": np.ascontiguousarray(np.concatenate(cols, axis=1)),
    }
    nc = bacc.Bacc("TRN2", target_bir_lowering=False, num_devices=1)
    aps = [nc.dram_tensor(n, a.shape, mybir.dt.from_np(a.dtype), kind="ExternalInput").ap() for n, a in arrays.items()]
    out = nc.dram_tensor("out_t", (CC, P, B * T), mybir.dt.float32, kind="ExternalOutput").ap()
    gates = nc.dram_tensor("gates_dram", (B * T // 512, E, 512), mybir.dt.float32, kind="Internal").ap()
    build_spiking_moe(nc, *aps, out, gates)
    r = run_bass_kernel_spmd(nc, [arrays], core_ids=[0])
    y = r.results[0]["out_t"]
    return np.ascontiguousarray(y.reshape(C, B, T).transpose(1, 2, 0))
```

```python
import concourse.bass as bass
from concourse import mybir
from contextlib import ExitStack

P = 128
T = 256
GT = 512
HALVES = 2
CHUNK = 1024


def expert_tiles(tokens, experts):
    tiles = 2 * tokens // P + experts - 1
    return tiles + tiles % 2


def build_spiking_moe(nc, x_t, cond_t, router_w, router_b, w_all, out, x1_cols, x1_rows, y_rows):
    F32 = mybir.dt.float32
    F32R = mybir.dt.float32r
    I32 = mybir.dt.int32
    U32 = mybir.dt.uint32
    ALU = mybir.AluOpType
    ACT = mybir.ActivationFunctionType
    AX = mybir.AxisListType

    CC, _, N = x_t.shape
    C = CC * P
    NB = cond_t.shape[2]
    E = router_b.shape[0]
    NG = N // GT
    HG = NG // HALVES
    BG = GT // T
    TT = GT // P
    NT = N // P
    HT = NT // HALVES
    SB = 4
    UP_S, DN_S, EXP = 0, 2 * CHUNK, 3 * CHUNK
    SHARED_CHUNKS = EXP // CHUNK
    NCHUNK = SHARED_CHUNKS + E
    TILES = expert_tiles(N // HALVES, E)
    STEPS = TILES // 2
    XR = 4
    PEEL = XR
    LOOPS = (STEPS - PEEL) // XR
    assert PEEL + LOOPS * XR == STEPS and LOOPS == HG and STEPS % 2 == 0
    UNITS = NT // 2
    DT = 0.001
    PER_SPIKE = 999.99993896484375
    THIRD = 1.0 / 3.0
    PS_COND = 2 * HT * E
    YR = 4
    HOTS = 8
    BATCHES = 2 * HT // HOTS
    INST = 2 * HT

    ctx = ExitStack()
    with ctx:
        def sb(name, shape, dt=F32):
            return ctx.enter_context(nc.sbuf_tensor(name, shape, dt))

        def sem(name):
            return ctx.enter_context(nc.semaphore(name))

        w_hi = sb("w_hi", [P, NCHUNK * CHUNK], F32R)
        w_lo = sb("w_lo", [P, NCHUNK * CHUNK], F32R)
        base = sb("base", [P, NT, C])
        w_raw_s = base[:, NT - 4 * SHARED_CHUNKS:NT, :].rearrange("p (k t) c -> p k (t c)", k=SHARED_CHUNKS)
        xg = sb("xg", [P, XR, 2, C])
        w_raw_e = xg[:, :, :, :].rearrange("p (k r) u c -> p k (r u c)", k=2)
        rw = sb("rw", [P, 2 * CC, E])
        rb = sb("rb", [P, E])
        cond = sb("cond", [P, CC, NB])
        cond_rw = sb("cond_rw", [P, CC, NB, E])
        cond_logit = sb("cond_logit", [P, NB, E])
        ones = sb("ones", [P, T])
        ident = sb("ident", [P, P])
        earlier = sb("earlier", [P, P])
        count = sb("count", [P, P])
        same_e = sb("same_e", [P, E, HT])
        tok = sb("tok", [P, 2, HT])
        x_in = sb("x_in", [P, CC, BG, T])
        init = sb("init", [P, CC, BG])
        x1 = sb("x1", [P, CC, GT])
        front = sb("front", [P, 4, BG * (T + 1) + 2])
        W1 = BG * (T + 1)
        rates = front[:, 0, 0:BG * T].rearrange("p (b t) -> p b t", b=BG)
        floors = front[:, 0, 0:W1].rearrange("p (b t) -> p b t", b=BG)
        sums = front[:, 1, 0:BG * T].rearrange("p (b t) -> p b t", b=BG)
        above = front[:, 1, 0:W1].rearrange("p (b t) -> p b t", b=BG)
        pot = front[:, 2, 0:W1].rearrange("p (b t) -> p b t", b=BG)
        spikes = front[:, 2, 0:BG * T].rearrange("p (b t) -> p b t", b=BG)
        pot_int = front[:, 3, 0:W1].rearrange("p (b t) -> p b t", b=BG).bitcast(I32)
        yv = [front[:, 2 * n:2 * n + 2, :].rearrange("p a b -> p (a b)")[:, 0:4 * C].rearrange(
            "p (q c) -> p q c", q=4) for n in range(2)]
        yv.append(x_in[:, :, :, :].rearrange("p c b t -> p (c b) t"))
        yv.append(x1[:, :, :].rearrange("p c n -> p (c n)").rearrange("p (q c) -> p q c", q=4))
        logit = sb("logit", [P, HT, E])
        score = sb("score", [P, HT, E])
        sel = logit
        top = sb("top", [P, HT, 8])
        top_i = sb("top_i", [P, HT, 8], U32)
        top_f = sb("top_f", [P, 2, HT])
        hot_s = sb("hot_s", [P, 2, HT, E])
        chosen = sb("chosen", [P, 2, HT])
        denom = sb("denom", [P, HT])
        denom_e = sb("denom_e", [P, HT])
        recip = sb("recip", [P, HT])
        big = sb("big", [P, HT])
        half = sb("half", [P, HT])
        recip_g = sb("recip_g", [P, HT])
        gate_m = sb("gate_m", [P, 2, HT])
        gate = sb("gate", [P, 2, NT])
        hot = sb("hot", [P, 2, HT, E])
        member = sb("member", [P, E, HT])
        prefix = sb("prefix", [P, E, HT])
        prefix_x = sb("prefix_x", [P, E, HT])
        n127 = sb("n127", [P, E], I32)
        n_tiles_i = sb("n_tiles_i", [P, E], I32)
        n_tiles = sb("n_tiles", [P, E])
        end_tile = sb("end_tile", [P, E])
        first_tile = sb("first_tile", [P, E])
        first_slot = sb("first_slot", [P, E])
        slot_e = prefix_x
        slot_f = sb("slot_f", [P, INST])
        slot_i = [sb(f"slot_i{h}", [P, INST], I32) for h in range(HALVES)]
        lane_i = sb("lane_i", [P, INST], I32)
        tile_i = sb("tile_i", [P, INST], I32)
        lane_f = sb("lane_f", [P, INST])
        tile_f = sb("tile_f", [P, INST])
        lane_hot = sb("lane_hot", [P, 2, HOTS, P], F32R)
        tile_hot = sb("tile_hot", [P, INST, TILES], F32R)
        tok_i = sb("tok_i", [P, TILES], I32)
        past_e = sb("past_e", [1, TILES, E])
        exp_f = sb("exp_f", [1, TILES])
        exp_i = [sb(f"exp_i{h}", [1, TILES], I32) for h in range(HALVES)]
        g_col = sb("g_col", [P, 2, 4], I32)
        c_col = sb("c_col", [P, YR, 4], I32)
        x_re = sb("x_re", [P, CC, GT])
        x_hi = sb("x_hi", [P, CC, GT], F32R)
        x_lo = sb("x_lo", [P, CC, GT], F32R)
        parts = sb("parts", [P, 8, GT], F32R)
        hid_hi, hid_lo = parts[:, 0:SB, :], parts[:, SB:2 * SB, :]
        xt_hi = [parts[:, n, :].rearrange("p (c s) -> p c s", c=CC) for n in (0, 1)]
        xt_lo = [parts[:, n, :].rearrange("p (c s) -> p c s", c=CC) for n in (2, 3)]
        ht_hi = [parts[:, n, :].rearrange("p (c s) -> p c s", c=CC) for n in (4, 5)]
        ht_lo = [parts[:, n, :].rearrange("p (c s) -> p c s", c=CC) for n in (6, 7)]
        works = sb("works", [P, 4, GT])
        act, hid = works[:, 0:2, :], works[:, 2:4, :]
        gelu, y_sb = works[:, 0:2, :], works[:, 2:4, :]

        ps = [ctx.enter_context(nc.psum_tensor(f"ps{n}", [P, GT], F32)) for n in range(4)]
        ps_d = [ctx.enter_context(nc.psum_tensor(f"ps_d{n}", [P, GT], F32)) for n in range(2)]
        ps_x, ps_h = [ps[0], ps_d[0]], [ps[2], ps_d[1]]
        ps_r = ctx.enter_context(nc.psum_tensor("ps_r", [P, GT], F32))
        ps_t = ctx.enter_context(nc.psum_tensor("ps_t", [P, GT], F32))

        s_w = [sem(f"w_loaded{n}") for n in range(NCHUNK)]
        s_small = sem("small_loaded")
        s_const = sem("const_made")
        s_whi = sem("w_hi_made")
        s_wlo = sem("w_lo_made")
        s_crw = sem("cond_rw_made")
        s_cl = sem("cond_logit_summed")
        s_clc = sem("cond_logit_kept")
        s_x = [sem(f"x_loaded{c}") for c in range(CC)]
        s_front = sem("front_step")
        s_logit = sem("logits_summed")
        s_score = sem("scores_made")
        s_xt = sem("x1_transposed")
        s_xev = sem("x1_rows_copied")
        s_xrow = [sem(f"x1_rows_stored{n}") for n in range(HG + 1)]
        s_xst = sem("x1_cols_stored")
        s_xre = sem("x1_cols_reloaded")
        s_xhi = sem("x_hi_made")
        s_xlo = sem("x_lo_made")
        s_place = sem("place_step")
        s_ranks = sem("ranks_summed")
        s_rate = sem("rates_made")
        s_int = sem("potentials_rounded")
        s_hot = sem("lane_one_hots_made")
        s_thot = sem("tile_one_hots_made")
        s_used = sem("one_hots_used")
        s_up = sem("up_done")
        s_act = sem("silu_made")
        s_hid = sem("hidden_made")
        s_hhi = sem("hid_hi_made")
        s_hlo = sem("hid_lo_made")
        s_down = sem("down_done")
        s_base = sem("base_made")
        s_xg = [sem(f"rows_gathered{n}") for n in range(XR)]
        s_gcol = sem("gather_columns_copied")
        s_ext = sem("exp_x_transposed")
        s_exhi = sem("exp_x_hi_made")
        s_exlo = sem("exp_x_lo_made")
        s_eup = sem("exp_up_done")
        s_ege = sem("exp_gelu_made")
        s_eht = sem("exp_h_transposed")
        s_ehhi = sem("exp_h_hi_made")
        s_ehlo = sem("exp_h_lo_made")
        s_edn = sem("exp_down_done")
        s_ey = sem("exp_y_copied")
        s_yst = [sem(f"y_stored{n}") for n in range(2)]
        s_ccol = sem("sum_columns_copied")
        s_yv = [sem(f"y_gathered{n}") for n in range(YR)]
        s_cmid = sem("first_choice_added")
        s_comb = sem("unit_summed")
        s_out = sem("out_stored")
        s_held = {e: sem(f"held_{e}") for e in ("sp", "act", "dve", "pool", "pe")}

        FRONT_STEPS = 18
        LOGIT_STEP, PREFIX_STEP = 1, 8 + 2 * HT
        TILE_STEP, TOKEN_STEP, EXPERT_STEP, PLACE_STEPS = 25 + 2 * HT, 26 + 2 * HT, 29 + 2 * HT, 40 + 2 * HT

        def after(engine, semaphore, value):
            if not (isinstance(value, int) and value <= 0):
                engine.wait_ge(semaphore, value)

        def hold(engine, name):
            engine.sem_inc(s_held[name], 1)

        def rows_stored(engine, h, g):
            engine.wait_ge(s_xrow[HG if h == 1 else g], 16 * HG if h == 1 else 16)

        def front_beside(k, i):
            if i is None:
                return HG if k < PEEL else None
            return None if i == LOOPS - 1 else HG + 1 + i

        def unit_beside(k, i):
            s = k if i is None else k + XR * i
            return s // 3 + 1 if s >= 3 and s % 3 == 0 and s // 3 + 1 < UNITS // 2 else None

        def turns(k, i, d):
            return k // d + (0 if i is None else i * (XR // d))

        def expert_phase(loop, step):
            for s in range(PEEL):
                step(s, s, None)
            for i in range(LOOPS):
                for k in range(XR):
                    step(PEEL + XR * i + k, PEEL + k, i)
            for s in range(STEPS, STEPS + 3):
                step(s, s, None)

        block = ctx.enter_context(nc.Block())

        @block.sync
        def _(sp):
            def load_x(g, c):
                after(sp, s_front, (g - 1) * FRONT_STEPS + (c + 1) * FRONT_STEPS // CC if not (isinstance(g, int) and g == 0) else 0)
                hold(sp, "sp")
                sp.dma_start(x_in[:, c, :, :].rearrange("p b t -> p (b t)"),
                             x_t[c, :, bass.ds(g * GT, GT)]).then_inc(s_x[c], 16)
                sp.dma_start(init[:, c, :], cond_t[:, c, bass.ds(g * BG, BG)]).then_inc(s_x[c], 16)

            def store_cols(g):
                sp.wait_ge(s_front, (g + 1) * FRONT_STEPS)
                hold(sp, "sp")
                sp.dma_start(x1_cols[bass.ds(g - HG, 1), :, :].rearrange("a p n -> p (a n)"),
                             x1[:, :, :].rearrange("p c n -> p (c n)")).then_inc(s_xst, 16)

            def store_rows(g, h):
                sp.wait_ge(s_xev, 2 * (g + 1))
                hold(sp, "sp")
                sp.dma_start(x1_rows[h][bass.ds((g - h * HG) * GT, GT), :].rearrange("(t p) c -> p t c", p=P),
                             base[:, bass.ds(g * TT, TT), :]).then_inc(s_xrow[HG if h == 1 else g], 16)

            def reload(g):
                sp.wait_ge(s_xst, 16 * (g - HG + 1))
                after(sp, s_xlo, g)
                hold(sp, "sp")
                sp.dma_start(x_re[:, :, :].rearrange("p c n -> p (c n)"),
                             x1_cols[bass.ds(g - HG, 1), :, :].rearrange("a p n -> p (a n)")).then_inc(s_xre, 16)

            def store_y(h, s, k):
                sp.wait_ge(s_ey, STEPS * h + s + 1)
                hold(sp, "sp")
                sp.dma_start(y_rows[h][bass.ds(s * 2 * P, 2 * P), :].rearrange("(u p) c -> p u c", p=P),
                             y_sb[:, k % 2, :].rearrange("p (u c) -> p u c", u=2)).then_inc(s_yst[k % 2], 16)

            def experts(h):
                def step(s, k, i):
                    if h == 0 and i is not None and k == PEEL and front_beside(k, i) is not None:
                        load_x(HG + 1 + i, 0)
                    if h == 0 and i is not None and k == PEEL + 1:
                        store_cols(HG + i)
                        if front_beside(k, i) is not None:
                            load_x(HG + 1 + i, 1)
                        else:
                            reload(HG)
                    if 3 <= k < STEPS + 3:
                        store_y(h, s - 3, k - 3)
                    if h == 0 and i is not None and k == PEEL + 3:
                        store_rows(HG + i, 1)
                    if h == 1 and (s < 2 or unit_beside(s - 2, None) is not None):
                        store_out(s if s < 2 else unit_beside(s - 2, None))
                expert_phase(nc.sync.Fori, step)

            def store_out(u):
                sp.wait_ge(s_comb, u + 1)
                sp.wait_ge(s_base, u + 1)
                hold(sp, "sp")
                sp.dma_start(out[bass.ds(u * 2 * P, 2 * P), :].rearrange("(t p) c -> p t c", p=P),
                             base[:, bass.ds(u * 2, 2), :]).then_inc(s_out, 16)

            load_x(0, 0)
            sp.dma_start(rw[:, :, :], router_w).then_inc(s_small, 16)
            sp.dma_start(cond[:, :, :], cond_t).then_inc(s_small, 16)
            sp.dma_start(rb[:, :], router_b.partition_broadcast(P)).then_inc(s_small, 16)
            load_x(0, 1)
            for k in range(SHARED_CHUNKS):
                sp.dma_start(w_raw_s[:, k, :], w_all[:, k * CHUNK:(k + 1) * CHUNK]).then_inc(s_w[k], 16)
            load_x(1, 0)
            load_x(1, 1)
            for g in range(HG):
                store_rows(g, 0)
                if g + 2 <= HG:
                    load_x(g + 2, 0)
                    load_x(g + 2, 1)
            experts(0)
            reload(HG + 1)
            reload(HG + 2)
            experts(1)
            reload(HG + 3)
            for u in range(UNITS // 2, UNITS):
                store_out(u)
            sp.wait_ge(s_out, 16 * UNITS)

        @block.gpsimd
        def _(pool):
            def load_w(k):
                if k >= SHARED_CHUNKS + 2:
                    pool.wait_ge(s_wlo, k - 1)
                nc.gpsimd.dma_start(w_raw_e[:, k % 2, :], w_all[:, k * CHUNK:(k + 1) * CHUNK]).then_inc(s_w[k], 16)

            nc.gpsimd.memset(ones[:, :], 1.0).then_inc(s_const, 1)
            nc.gpsimd.memset(ident[:, :], 0.0).then_inc(s_const, 1)
            nc.gpsimd.memset(earlier[:, :], 1.0).then_inc(s_const, 1)
            nc.gpsimd.memset(same_e[:, :, :], 1.0).then_inc(s_const, 1)
            nc.gpsimd.iota(count[:, :], pattern=[[1, P]], base=0, channel_multiplier=0,
                           allow_small_or_imprecise_dtypes=True).then_inc(s_const, 1)
            nc.gpsimd.iota(tok[:, :, :], pattern=[[0, 2], [P, HT]], base=0, channel_multiplier=1,
                           allow_small_or_imprecise_dtypes=True).then_inc(s_const, 1)
            pool.wait_ge(s_const, 6)
            nc.gpsimd.affine_select(out=ident[:, :], in_=ident[:, :], compare_op=ALU.not_equal, fill=1.0,
                                    base=0, pattern=[[-1, P]], channel_multiplier=1).then_inc(s_const, 1)
            nc.gpsimd.affine_select(out=earlier[:, :], in_=earlier[:, :], compare_op=ALU.is_gt, fill=0.0,
                                    base=0, pattern=[[1, P]], channel_multiplier=-1).then_inc(s_const, 1)
            nc.gpsimd.memset(same_e[:, :, 0:1], 0.0).then_inc(s_const, 1)
            for k in range(NCHUNK):
                cols = slice(k * CHUNK, (k + 1) * CHUNK)
                raw = w_raw_s[:, k, :] if k < SHARED_CHUNKS else w_raw_e[:, k % 2, :]
                pool.wait_ge(s_w[k], 16)
                pool.wait_ge(s_whi, k + 1)
                nc.gpsimd.tensor_tensor(w_lo[:, cols], raw, w_hi[:, cols].bitcast(F32), ALU.subtract).then_inc(s_wlo, 1)
                if SHARED_CHUNKS <= k < NCHUNK - 2:
                    load_w(k + 2)
                if k == 0:
                    load_w(SHARED_CHUNKS)
                    load_w(SHARED_CHUNKS + 1)

            def gather(h, s, k, i):
                if k % 2 == 0:
                    for r in range(2):
                        after(pool, s_xg[k % XR + r], 2 * 16 * (STEPS // XR * h + turns(k, i, XR)))
                    hold(pool, "pool")
                    nc.gpsimd.tensor_copy(g_col[:, k // 2 % 2, :], tok_i[:, bass.ds(2 * s, 4)]).then_inc(s_gcol, 1)
                    pool.wait_ge(s_gcol, STEPS // 2 * h + turns(k, i, 2) + 1)
                after(pool, s_ext, STEPS * h + s - XR + 1)
                hold(pool, "pool")
                for u in range(2):
                    c = 2 * (k % 2) + u
                    nc.gpsimd.indirect_dma_start(
                        xg[:, k % XR, u, :], None, x1_rows[h],
                        bass.IndirectOffsetOnAxis(ap=g_col[:, k // 2 % 2, c:c + 1], axis=0)).then_inc(s_xg[k % XR], 16)

            def gather_y(h, u):
                par = u % YR
                after(pool, s_comb, u - YR + 1)
                hold(pool, "pool")
                nc.gpsimd.tensor_copy(c_col[:, par, :].rearrange("p (t k) -> p k t", k=2),
                                      slot_i[h][:, :].rearrange("p (k t) -> p k t", k=2)[:, :, bass.ds(2 * u - h * HT, 2)]
                                      ).then_inc(s_ccol, 1)
                pool.wait_ge(s_ccol, u + 1)
                hold(pool, "pool")
                for q in range(4):
                    nc.gpsimd.indirect_dma_start(
                        yv[par][:, q, :], None, y_rows[h],
                        bass.IndirectOffsetOnAxis(ap=c_col[:, par, q:q + 1], axis=0)).then_inc(s_yv[par], 16)

            def tile_hots(h):
                pool.wait_ge(s_place, h * PLACE_STEPS + TILE_STEP - 1)
                nc.gpsimd.tensor_tensor(tile_hot[:, HT:, :], tile_hot[:, HT:, :].bitcast(F32),
                                        tok[:, 1, :].unsqueeze(2).to_broadcast([P, HT, TILES]), ALU.mult).then_inc(s_thot, 1)

            def y_rows_stored(h):
                for n in range(2):
                    pool.wait_ge(s_yst[n], 16 * (h + 1) * STEPS // 2)

            def experts(h):
                pool.wait_ge(s_place, h * PLACE_STEPS + TOKEN_STEP)
                for g in range(HG):
                    rows_stored(pool, h, g)
                def step(s, k, i):
                    if k < STEPS:
                        gather(h, s, k, i)
                    if h == 1 and unit_beside(k, i) is not None:
                        gather_y(0, unit_beside(k, i))
                expert_phase(nc.gpsimd.Fori, step)

            pool.wait_ge(s_wlo, NCHUNK)
            tile_hots(0)
            experts(0)
            tile_hots(1)
            y_rows_stored(0)
            pool.wait_ge(s_front, NG * FRONT_STEPS)
            pool.wait_ge(s_logit, NG)
            pool.wait_ge(s_xt, 2 * NG)
            pool.wait_ge(s_xst, 16 * HG)
            gather_y(0, 0)
            gather_y(0, 1)
            experts(1)
            y_rows_stored(1)
            for u in range(UNITS // 2, UNITS):
                gather_y(1, u)

        @block.scalar
        def _(act_e):
            def split(g, half):
                if half == 0:
                    act_e.wait_ge(s_front, (g + 1) * FRONT_STEPS)
                else:
                    act_e.wait_ge(s_xre, 16 * (g - HG + 1))
                after(act_e, s_up, g * SB)
                after(act_e, s_xlo, g)
                nc.scalar.activation(x_hi[:, :, :], (x1 if half == 0 else x_re)[:, :, :], ACT.Copy).then_inc(s_xhi, 1)

            def copy_rows(g, r):
                act_e.wait_ge(s_xt, 2 * g + r + 1)
                hold(act_e, "act")
                nc.scalar.activation(base[:, bass.ds(g * TT + 2 * r, 2), :].rearrange("p t c -> p (t c)"),
                                     ps_t[:, :], ACT.Copy).then_inc(s_xev, 1)

            n_front = FRONT_STEPS // CC

            def split_w(k):
                act_e.wait_ge(s_w[k], 16)
                raw = w_raw_s[:, k, :] if k < SHARED_CHUNKS else w_raw_e[:, k % 2, :]
                nc.scalar.activation(w_hi[:, k * CHUNK:(k + 1) * CHUNK], raw, ACT.Copy).then_inc(s_whi, 1)

            def scores(h):
                act_e.wait_ge(s_place, h * PLACE_STEPS + LOGIT_STEP)
                nc.scalar.activation(score[:, :, :], logit[:, :, :], ACT.Sigmoid).then_inc(s_score, 1)

            def rates_of(g, c):
                act_e.wait_ge(s_x[c], 32 * (g + 1))
                after(act_e, s_front, g * FRONT_STEPS + c * n_front - 1)
                nc.scalar.activation(rates, x_in[:, c, :, :], ACT.Relu, scale=DT).then_inc(s_rate, 1)

            def rounded(g, c):
                act_e.wait_ge(s_front, g * FRONT_STEPS + c * n_front + 5)
                nc.scalar.activation(pot_int, pot, ACT.Copy).then_inc(s_int, 1)

            def shared(g, ahead):
                if 0 < g and g + 1 < HG:
                    rounded(g + 1, 1)
                for b in range(SB):
                    act_e.wait_ge(s_up, g * SB + b + 1)
                    after(act_e, s_hid, g * SB + b - 1)
                    nc.scalar.activation(act[:, b % 2, :], ps[2 * (b % 2)][:, :], ACT.Silu).then_inc(s_act, 1)
                    if g + 2 < HG and b == 2:
                        rounded(g + 2, 0)
                    act_e.wait_ge(s_hid, g * SB + b + 1)
                    after(act_e, s_down, g * SB + b + 1 - SB)
                    nc.scalar.activation(hid_hi[:, b, :], hid[:, b % 2, :], ACT.Copy).then_inc(s_hhi, 1)
                    if g == 0 and b == 0:
                        rounded(1, 1)
                    if g + 2 < HG and b == 1:
                        rates_of(g + 2, 0)
                    if g < HG - 1 and b < 3 and SHARED_CHUNKS + 3 * g + b < NCHUNK:
                        split_w(SHARED_CHUNKS + 3 * g + b)
                if ahead is not None:
                    split(ahead, ahead // HG)
                    if ahead == HG - 1:
                        scores(0)
                    if g + 2 < HG:
                        rates_of(g + 2, 1)
                    if ahead < HG:
                        copy_rows(ahead, 0)
                        copy_rows(ahead, 1)

            def experts(h):
                def step(s, k, i):
                    S = STEPS * h + s
                    if h == 0 and k == STEPS + 1:
                        split(HG, 1)
                    if k < STEPS:
                        act_e.wait_ge(s_ext, S + 1)
                        after(act_e, s_eup, S - 1)
                        nc.scalar.activation(xt_hi[k % 2].rearrange("p c s -> p (c s)"), ps_x[k % 2][:, :],
                                             ACT.Copy).then_inc(s_exhi, 1)
                    if h == 0 and i is not None and k >= PEEL + 2:
                        copy_rows(HG + i, k - PEEL - 2)
                    if 1 <= k <= STEPS:
                        act_e.wait_ge(s_eup, S)
                        after(act_e, s_eht, S - 2)
                        nc.scalar.activation(gelu[:, (k - 1) % 2, :], ps[1][:, :], ACT.Gelu).then_inc(s_ege, 1)
                    if h == 0 and i is not None and k == PEEL:
                        rounded(HG + i, 1)
                    elif h == 0 and k % XR and front_beside(k, i) is not None:
                        if k % XR == 2:
                            rounded(front_beside(k, i), 0)
                        else:
                            rates_of(front_beside(k, i), k % XR // 2)
                    if 2 <= k <= STEPS + 1:
                        act_e.wait_ge(s_eht, S - 1)
                        after(act_e, s_edn, S - 3)
                        nc.scalar.activation(ht_hi[k % 2].rearrange("p c s -> p (c s)"), ps_h[k % 2][:, :],
                                             ACT.Copy).then_inc(s_ehhi, 1)
                    if 3 <= k:
                        act_e.wait_ge(s_edn, S - 2)
                        after(act_e, s_yst[(k - 3) % 2], 16 * (STEPS // 2 * h + turns(k - 3, i, 2)))
                        nc.scalar.activation(y_sb[:, (k - 3) % 2, :], ps[3][:, :], ACT.Copy).then_inc(s_ey, 1)
                    if h == 0 and i == LOOPS - 1 and k == PEEL + 2:
                        scores(1)
                expert_phase(nc.scalar.Fori, step)

            rates_of(0, 0)
            rounded(0, 0)
            rates_of(0, 1)
            split_w(0)
            rounded(0, 1)
            split_w(1)
            split_w(2)
            split(0, 0)
            copy_rows(0, 0)
            copy_rows(0, 1)
            act_e.wait_ge(s_cl, 1)
            nc.scalar.activation(cond_logit[:, :, :].rearrange("p b e -> p (b e)"), ps_r[:, PS_COND:PS_COND + NB * E],
                                 ACT.Copy).then_inc(s_clc, 1)
            rates_of(1, 0)
            rounded(1, 0)
            rates_of(1, 1)
            for g in range(HG - 1):
                shared(g, g + 1)
            shared(HG - 1, None)
            act_e.wait_ge(s_down, HG * SB)
            act_e.wait_ge(s_hlo, HG * SB)
            act_e.wait_ge(s_wlo, SHARED_CHUNKS)
            experts(0)
            act_e.wait_ge(s_eht, STEPS)
            act_e.wait_ge(s_edn, STEPS)
            shared(HG, HG + 1)
            act_e.wait_ge(s_down, (HG + 1) * SB)
            act_e.wait_ge(s_hlo, (HG + 1) * SB)
            experts(1)
            act_e.wait_ge(s_eht, 2 * STEPS)
            act_e.wait_ge(s_edn, 2 * STEPS)
            shared(HG + 1, HG + 2)
            shared(HG + 2, HG + 3)
            shared(HG + 3, None)

        @block.vector
        def _(dve):
            def front_steps(g, xst=None):
                n = FRONT_STEPS // CC

                def done(ins):
                    ins.then_inc(s_front, 1)

                def chunk(c):
                    def need(k):
                        dve.wait_ge(s_front, g * FRONT_STEPS + c * n + k)

                    def start_col():
                        after(dve, s_front, g * FRONT_STEPS + c * n)
                        dve.wait_ge(s_x[c], 32 * (g + 1))
                        done(nc.vector.tensor_scalar(pot[:, :, 0], init[:, c, :], 0.0, None, ALU.add))

                    def scan(b):
                        dve.wait_ge(s_rate, CC * g + c + 1)
                        done(nc.vector.tensor_tensor_scan(sums[:, b, :], ones[:, :], rates[:, b, :], 0.0,
                                                          ALU.mult, ALU.add))

                    def add_init(b):
                        need(2 + b)
                        done(nc.vector.tensor_scalar(pot[:, b, 1:T + 1], sums[:, b, :], init[:, c, b:b + 1],
                                                     None, ALU.add))

                    def rounded_up():
                        dve.wait_ge(s_int, CC * g + c + 1)
                        done(nc.vector.tensor_tensor(above, pot_int, pot, ALU.is_gt))

                    def floor():
                        need(6)
                        done(nc.vector.tensor_tensor(floors, pot_int, above, ALU.subtract))

                    def spike():
                        need(7)
                        done(nc.vector.tensor_tensor(spikes, floors[:, :, 1:T + 1], floors[:, :, 0:T], ALU.subtract))

                    def new_x1():
                        need(8)
                        if c == 0:
                            after(dve, s_logit, g)
                            after(dve, s_xt, 2 * g)
                            if xst is None:
                                after(dve, s_xhi, g)
                                after(dve, s_xlo, g)
                            else:
                                dve.wait_ge(s_xst, 16 * xst)
                        done(nc.vector.scalar_tensor_tensor(
                            x1[:, c, :].rearrange("p (b t) -> p b t", b=BG), spikes,
                            PER_SPIKE, x_in[:, c, :, :], ALU.mult, ALU.add))

                    return [start_col, lambda: scan(0), lambda: scan(1), lambda: add_init(0),
                            lambda: add_init(1), rounded_up, floor, spike, new_x1]

                steps = chunk(0) + chunk(1)
                assert len(steps) == FRONT_STEPS
                return steps

            def place_steps(h):
                n = [0]
                base_n = h * PLACE_STEPS

                def done(ins):
                    n[0] += 1
                    ins.then_inc(s_place, 1)

                def need_last():
                    dve.wait_ge(s_place, base_n + n[0])

                def flat(t):
                    return t[:, :, :].rearrange("p a b -> p (a b)")

                def over(t, k):
                    return t[:, :, k:k + 1].to_broadcast([P, HT, E])

                def choose():
                    dve.wait_ge(s_logit, (h + 1) * HG)
                    done(nc.vector.tensor_tensor(
                        logit[:, :, :].rearrange("p (b t) e -> p b t e", t=T // P),
                        ps_r[:, 0:HT * E].rearrange("p (b t e) -> p b t e", t=T // P, e=E),
                        cond_logit[:, h * NB // HALVES:(h + 1) * NB // HALVES, :].unsqueeze(2)
                        .to_broadcast([P, NB // HALVES, T // P, E]), ALU.add))
                    assert n[0] == LOGIT_STEP

                def top_two():
                    dve.wait_ge(s_score, h + 1)
                    done(nc.vector.tensor_tensor(sel[:, :, :], score[:, :, :],
                                                 rb[:, :].unsqueeze(1).to_broadcast([P, HT, E]), ALU.add))
                    need_last()
                    hold(dve, "dve")
                    for t in range(HT):
                        done(nc.vector.max(top[:, t, :], sel[:, t, :]))
                    need_last()
                    hold(dve, "dve")
                    for t in range(HT):
                        done(nc.vector.max_index(top_i[:, t, :], top[:, t, :], sel[:, t, :]))
                    need_last()
                    done(nc.vector.tensor_copy(top_f[:, :, :].rearrange("p k t -> p t k"), top_i[:, :, 0:2]))
                    need_last()
                    for k in range(2):
                        done(nc.vector.tensor_tensor(hot[:, k, :, :],
                                                     count[:, 0:E].unsqueeze(1).to_broadcast([P, HT, E]),
                                                     top_f[:, k, :].unsqueeze(2).to_broadcast([P, HT, E]),
                                                     ALU.is_equal))
                    need_last()

                def prefixes():
                    done(nc.vector.tensor_tensor(member[:, :, :], hot[:, 0, :, :].rearrange("p t e -> p e t"),
                                                 hot[:, 1, :, :].rearrange("p t e -> p e t"), ALU.add))
                    need_last()
                    done(nc.vector.tensor_tensor_scan(flat(prefix), flat(same_e), flat(member), 0.0,
                                                      ALU.mult, ALU.add))
                    need_last()
                    done(nc.vector.tensor_tensor(prefix_x[:, :, :], prefix[:, :, :], member[:, :, :], ALU.subtract))
                    assert n[0] == PREFIX_STEP, n[0]

                def gates():
                    for k in range(2):
                        done(nc.vector.tensor_tensor(hot_s[:, k, :, :], hot[:, k, :, :], score[:, :, :], ALU.mult))
                    need_last()
                    done(nc.vector.tensor_reduce(chosen[:, :, :], hot_s[:, :, :, :], axis=AX.X, op=ALU.add))
                    need_last()
                    done(nc.vector.tensor_tensor(denom[:, :], chosen[:, 0, :], chosen[:, 1, :], ALU.add))
                    need_last()
                    done(nc.vector.tensor_scalar(denom_e[:, :], denom[:, :], 1e-9, None, ALU.add))
                    done(nc.vector.tensor_scalar(big[:, :], denom[:, :], 1e-9, None, ALU.is_gt))
                    need_last()
                    done(nc.vector.reciprocal(recip[:, :], denom_e[:, :]))
                    done(nc.vector.tensor_scalar(half[:, :], big[:, :], -0.5 * THIRD, 0.5 * THIRD, ALU.mult, ALU.add))
                    need_last()
                    done(nc.vector.scalar_tensor_tensor(recip_g[:, :], recip[:, :], THIRD, big[:, :],
                                                        ALU.mult, ALU.mult))
                    need_last()
                    done(nc.vector.tensor_tensor(gate_m[:, :, :], chosen[:, :, :],
                                                 recip_g[:, :].unsqueeze(1).to_broadcast([P, 2, HT]), ALU.mult))
                    need_last()
                    done(nc.vector.tensor_tensor(gate[:, :, h * HT:(h + 1) * HT], gate_m[:, :, :],
                                                 half[:, :].unsqueeze(1).to_broadcast([P, 2, HT]), ALU.add))
                    assert n[0] == PLACE_STEPS, n[0]

                def slots():
                    dve.wait_ge(s_ranks, h + 1)
                    done(nc.vector.tensor_scalar(n127[:, :], ps_r[:, 2 * HT * E:2 * HT * E + E], P - 1.0, None, ALU.add))
                    need_last()
                    done(nc.vector.tensor_scalar(n_tiles_i[:, :], n127[:, :], 7, None, ALU.logical_shift_right))
                    need_last()
                    done(nc.vector.tensor_copy(n_tiles[:, :], n_tiles_i[:, :]))
                    need_last()
                    done(nc.vector.tensor_tensor_scan(end_tile[:, :], ones[:, 0:E], n_tiles[:, :], 0.0,
                                                      ALU.mult, ALU.add))
                    need_last()
                    done(nc.vector.tensor_tensor(first_tile[:, :], end_tile[:, :], n_tiles[:, :], ALU.subtract))
                    need_last()
                    done(nc.vector.tensor_scalar(first_slot[:, :], first_tile[:, :], float(P), None, ALU.mult))
                    need_last()
                    done(nc.vector.tensor_tensor(slot_e[:, :, :],
                                                 ps_r[:, HT * E:2 * HT * E].rearrange("p (e t) -> p e t", e=E),
                                                 first_slot[:, :].unsqueeze(2).to_broadcast([P, E, HT]), ALU.add))
                    need_last()
                    for k in range(2):
                        done(nc.vector.tensor_tensor(hot_s[:, k, :, :], hot[:, k, :, :],
                                                     slot_e[:, :, :].rearrange("p e t -> p t e"), ALU.mult))
                    need_last()
                    done(nc.vector.tensor_reduce(slot_f[:, :].rearrange("p (k t) -> p k t", k=2), hot_s[:, :, :, :],
                                                 axis=AX.X, op=ALU.add))
                    need_last()
                    done(nc.vector.tensor_copy(slot_i[h][:, :], slot_f[:, :]))
                    need_last()
                    done(nc.vector.tensor_scalar(lane_i[:, :], slot_i[h][:, :], P - 1, None, ALU.bitwise_and))
                    done(nc.vector.tensor_scalar(tile_i[:, :], slot_i[h][:, :], 7, None, ALU.logical_shift_right))
                    need_last()
                    done(nc.vector.tensor_copy(lane_f[:, :], lane_i[:, :]))
                    done(nc.vector.tensor_copy(tile_f[:, :], tile_i[:, :]))
                    need_last()

                def tile_hots():
                    done(nc.vector.tensor_tensor(tile_hot[:, :, :], count[:, 0:TILES].unsqueeze(1).to_broadcast([P, INST, TILES]),
                                                 tile_f[:, :].unsqueeze(2).to_broadcast([P, INST, TILES]), ALU.is_equal))
                    need_last()
                    done(nc.vector.tensor_tensor(tile_hot[:, 0:HT, :], tile_hot[:, 0:HT, :].bitcast(F32),
                                                 tok[:, 0, :].unsqueeze(2).to_broadcast([P, HT, TILES]), ALU.mult))
                    assert n[0] == TILE_STEP, n[0]

                def lane_hots(b):
                    after(dve, s_used, h * BATCHES + b - 1)
                    nc.vector.tensor_tensor(lane_hot[:, b % 2, :, :], count[:, :].unsqueeze(1).to_broadcast([P, HOTS, P]),
                                            lane_f[:, b * HOTS:(b + 1) * HOTS].unsqueeze(2).to_broadcast([P, HOTS, P]),
                                            ALU.is_equal).then_inc(s_hot, 1)

                def tokens():
                    dve.wait_ge(s_used, (h + 1) * BATCHES)
                    after(dve, s_gcol, h * STEPS // 2)
                    done(nc.vector.tensor_copy(tok_i[:, :], ps_t[:, 0:TILES]))
                    assert n[0] == TOKEN_STEP, n[0]

                def tile_experts():
                    done(nc.vector.tensor_tensor(past_e[:, :, :], count[0:1, 0:TILES].unsqueeze(2).to_broadcast([1, TILES, E]),
                                                 end_tile[0:1, :].unsqueeze(1).to_broadcast([1, TILES, E]), ALU.is_ge))
                    need_last()
                    done(nc.vector.tensor_reduce(exp_f[:, :], past_e[:, :, :], axis=AX.X, op=ALU.add))
                    need_last()
                    done(nc.vector.tensor_scalar(exp_i[h][:, :], exp_f[:, :], E - 1.0, float(CHUNK),
                                                 ALU.min, ALU.mult))
                    assert n[0] == EXPERT_STEP, n[0]

                lanes = [lambda b=b: lane_hots(b) for b in range(BATCHES)]
                return [choose, top_two, prefixes, slots, tile_hots, *lanes, tokens, tile_experts, gates]

            def unit_steps(u, first=False):
                par, seen = u % YR, u // YR + 1
                def add(k):
                    if k == 0:
                        if first:
                            rows_stored(dve, 1, u // 2)
                        else:
                            dve.wait_ge(s_base, 2 * (u // 2 + 1))
                        dve.wait_ge(s_yv[par], 4 * 16 * seen)
                    else:
                        dve.wait_ge(s_cmid, u + 1)
                    for t in range(2):
                        tile = base[:, bass.ds(2 * u + t, 1), :].rearrange("p a c -> p (a c)")
                        last = nc.vector.scalar_tensor_tensor(
                            tile, yv[par][:, 2 * t + k, :],
                            gate[:, k, bass.ds(2 * u + t, 1)],
                            tile, ALU.mult, ALU.add)
                    last.then_inc(s_cmid if k == 0 else s_comb, 1)
                return [lambda: add(0), lambda: add(1)]

            def units(a, b):
                return [f for u in range(a, b) for f in unit_steps(u)]

            def split(g, half):
                dve.wait_ge(s_xhi, g + 1)
                nc.vector.tensor_tensor(x_lo[:, :, :], (x1 if half == 0 else x_re)[:, :, :],
                                        x_hi[:, :, :].bitcast(F32), ALU.subtract).then_inc(s_xlo, 1)

            def finish(g, units_added=0):
                after(dve, s_comb, units_added)
                dve.wait_ge(s_down, (g + 1) * SB)
                rows_stored(dve, g // HG, g)
                for d in range(2):
                    rows = base[:, bass.ds(g * TT + 2 * d, 2), :].rearrange("p t c -> p (t c)")
                    nc.vector.scalar_tensor_tensor(rows, ps_d[d][:, :], THIRD, rows,
                                                   ALU.mult, ALU.add).then_inc(s_base, 1)

            def shared(g, fill, ahead, half, behind=None, units_added=0):
                for f in fill[0]:
                    f()
                if behind is not None:
                    finish(behind, units_added)
                for b in range(SB):
                    dve.wait_ge(s_act, g * SB + b + 1)
                    after(dve, s_hhi, g * SB + b - 1)
                    after(dve, s_hlo, g * SB + b - 1)
                    nc.vector.tensor_tensor(hid[:, b % 2, :], act[:, b % 2, :], ps[2 * (b % 2) + 1][:, :],
                                            ALU.mult).then_inc(s_hid, 1)
                    early = 1 if g < HG - 1 else 0
                    for f in fill[b + 1][0:early]:
                        f()
                    dve.wait_ge(s_hhi, g * SB + b + 1)
                    after(dve, s_down, g * SB + b + 1 - SB)
                    nc.vector.tensor_tensor(hid_lo[:, b, :], hid[:, b % 2, :], hid_hi[:, b, :].bitcast(F32),
                                            ALU.subtract).then_inc(s_hlo, 1)
                    if b == SB - 1 and ahead is not None:
                        split(ahead, half)
                    for f in fill[b + 1][early:]:
                        f()

            def spread(steps, shares):
                lists, at = [], 0
                for n in shares:
                    lists.append(steps[at:at + n])
                    at += n
                assert at >= len(steps)
                return lists

            def experts(h):
                def step(s, k, i):
                    S = STEPS * h + s
                    if h == 0 and k == STEPS + 1:
                        split(HG, 1)
                    if k < STEPS:
                        dve.wait_ge(s_exhi, S + 1)
                        after(dve, s_eup, S - 1)
                        nc.vector.tensor_tensor(xt_lo[k % 2].rearrange("p c s -> p (c s)"), ps_x[k % 2][:, :],
                                                xt_hi[k % 2].rearrange("p c s -> p (c s)").bitcast(F32),
                                                ALU.subtract).then_inc(s_exlo, 1)
                    if 2 <= k <= STEPS + 1:
                        dve.wait_ge(s_ehhi, S - 1)
                        after(dve, s_edn, S - 3)
                        nc.vector.tensor_tensor(ht_lo[k % 2].rearrange("p c s -> p (c s)"), ps_h[k % 2][:, :],
                                                ht_hi[k % 2].rearrange("p c s -> p (c s)").bitcast(F32),
                                                ALU.subtract).then_inc(s_ehlo, 1)
                    n = (0, 5, 8, 14, FRONT_STEPS)
                    if h == 0 and i is not None and k == PEEL:
                        for f in front_steps(HG + i, 1)[n[3]:]:
                            f()
                    if h == 0 and k % XR and front_beside(k, i) is not None:
                        for f in front_steps(front_beside(k, i), None if i is None else i + 1)[n[k % XR - 1]:n[k % XR]]:
                            f()
                    if h == 0 and i == LOOPS - 1 and k >= PEEL + 2:
                        place[1][k - PEEL - 2]()
                    if h == 0 and k in (STEPS, STEPS + 2):
                        place[1][2 + (k - STEPS) // 2]()
                    if h == 1 and (s < 2 or unit_beside(s - 2, None) is not None):
                        for f in unit_steps(s if s < 2 else unit_beside(s - 2, None)):
                            f()
                expert_phase(nc.vector.Fori, step)

            dve.wait_ge(s_const, 9)
            fronts = [f for g in range(HG) for f in front_steps(g)]
            lead = FRONT_STEPS + FRONT_STEPS // CC - 1
            for f in fronts[0:FRONT_STEPS]:
                f()
            split(0, 0)
            dve.wait_ge(s_small, 16 * 3)
            for c in range(CC):
                nc.vector.tensor_tensor(cond_rw[:, c, :, :], cond[:, c, :].unsqueeze(2).to_broadcast([P, NB, E]),
                                        rw[:, CC + c, :].unsqueeze(1).to_broadcast([P, NB, E]),
                                        ALU.mult).then_inc(s_crw, 1)
            for f in fronts[FRONT_STEPS:lead]:
                f()
            for g in range(HG - 1):
                todo = fronts[lead + g * FRONT_STEPS:lead + (g + 1) * FRONT_STEPS]
                shared(g, spread(todo, (6, 4, 5, 3, 0) if g > 0 else (0, 6, 9, 3, 0)), g + 1, 0, g - 1 if g > 0 else None)
            dve.wait_ge(s_clc, 1)
            place = [place_steps(h) for h in range(HALVES)]
            p = place[0]
            shared(HG - 1, [[p[0], p[1], p[2], lambda: finish(HG - 2)], p[3:4], p[4:10], p[10:11], p[11:]], None, 0)
            finish(HG - 1)
            experts(0)
            p = place[1]
            for f in p[4:7]:
                f()
            for n in range(2):
                dve.wait_ge(s_yst[n], 16 * STEPS // 2)
            shared(HG, [[], p[7:9], p[9:11], p[11:], []], HG + 1, 1)
            finish(HG)
            experts(1)
            for n in range(2):
                dve.wait_ge(s_yst[n], 2 * 16 * STEPS // 2)
            shared(HG + 1, [[], [], [], [], units(8, 10)], HG + 2, 1)
            shared(HG + 2, [[], [], units(10, 11), units(11, 12), unit_steps(12, True)], HG + 3, 1, HG + 1)
            shared(HG + 3, [[], units(13, 14), unit_steps(14, True), [], unit_steps(15, True)], None, 1, HG + 2, 13)
            finish(HG + 3, UNITS)

        @block.tensor
        def _(pe):
            def three(out, x_hi, x_lo, w_hi, w_lo, start, stop):
                nc.tensor.matmul(out, x_hi, w_hi, start=start, stop=False, skip_group_check=True)
                nc.tensor.matmul(out, x_lo, w_hi, start=False, stop=False, skip_group_check=True)
                return nc.tensor.matmul(out, x_hi, w_lo, start=False, stop=stop, skip_group_check=True)

            def up(g, b):
                after(pe, s_hid, g * SB + b - 1)
                for half in range(2):
                    for c in range(CC):
                        col = UP_S + ((b * 2 + half) * CC + c) * P
                        wh, wl = w_hi[:, col:col + P], w_lo[:, col:col + P]
                        last = three(ps[2 * (b % 2) + half][:, :], wh, wl, x_hi[:, c, :], x_lo[:, c, :],
                                     c == 0, c == CC - 1)
                last.then_inc(s_up, 1)

            def down(g, b):
                pe.wait_ge(s_hhi, g * SB + b + 1)
                pe.wait_ge(s_hlo, g * SB + b + 1)
                if b == 0:
                    after(pe, s_base, 2 * g)
                col = DN_S + b * C
                for t in range(TT):
                    toks = slice(t * P, (t + 1) * P)
                    last = three(ps_d[t // 2][:, (t % 2) * C:(t % 2 + 1) * C], hid_hi[:, b, toks], hid_lo[:, b, toks],
                                 w_hi[:, col:col + C], w_lo[:, col:col + C], b == 0 and t % 2 == 0, b == SB - 1)
                last.then_inc(s_down, 1)

            def logits(g, n):
                pe.wait_ge(s_front, (g + 1) * FRONT_STEPS)
                for t in range(TT):
                    for c in range(CC):
                        last = nc.tensor.matmul(ps_r[:, bass.ds(n * TT * E + t * E, E)], x1[:, c, t * P:(t + 1) * P],
                                                rw[:, c, :], start=(c == 0), stop=(c == CC - 1))
                last.then_inc(s_logit, 1)

            def to_rows(g, r):
                after(pe, s_xev, 2 * g + r)
                for t in range(2):
                    for c in range(CC):
                        n = (2 * r + t) * P
                        last = nc.tensor.transpose(ps_t[:, t * C + c * P:t * C + (c + 1) * P], x1[:, c, n:n + P],
                                                   ident[:, :])
                last.then_inc(s_xt, 1)

            def ranks(h):
                pe.wait_ge(s_place, h * PLACE_STEPS + PREFIX_STEP)
                dst = ps_r[:, HT * E:2 * HT * E]
                nc.tensor.matmul(dst, earlier[:, :], member[:, :, :].rearrange("p e t -> p (e t)"), start=True, stop=False)
                nc.tensor.matmul(dst, ones[:, 0:P], prefix_x[:, :, :].rearrange("p e t -> p (e t)"), start=False, stop=True)
                nc.tensor.matmul(ps_r[:, 2 * HT * E:2 * HT * E + E], ones[:, 0:P], prefix[:, :, HT - 1],
                                 start=True, stop=True).then_inc(s_ranks, 1)

            def slot_tokens(h, a, b):
                pe.wait_ge(s_xev, 2 * HG * (h + 1))
                pe.wait_ge(s_place, h * PLACE_STEPS + TILE_STEP)
                for n in range(a, b):
                    pe.wait_ge(s_hot, h * BATCHES + n + 1)
                    if n == BATCHES // 2:
                        pe.wait_ge(s_thot, h + 1)
                    for j in range(n * HOTS, (n + 1) * HOTS):
                        last = nc.tensor.matmul(ps_t[:, 0:TILES], lane_hot[:, n % 2, j % HOTS, :], tile_hot[:, j, :],
                                                start=(j == 0), stop=(j == INST - 1))
                    last.then_inc(s_used, 1)

            def cond_products():
                pe.wait_ge(s_small, 16 * 3)
                pe.wait_ge(s_crw, CC)
                for c in range(CC):
                    last = nc.tensor.matmul(ps_r[:, PS_COND:PS_COND + NB * E], ones[:, 0:P],
                                            cond_rw[:, c, :, :].rearrange("p b e -> p (b e)"),
                                            start=(c == 0), stop=(c == CC - 1))
                last.then_inc(s_cl, 1)
                pe.wait_ge(s_clc, 1)

            def shared(g, ahead=None, h=None):
                pe.wait_ge(s_xlo, g + 1)
                if g == 0:
                    pe.wait_ge(s_wlo, SHARED_CHUNKS)
                if g not in (HG, HG + 1):
                    up(g, 0)
                if g == HG - 1:
                    to_rows(g, 1)
                if g == 0:
                    logits(0, 0)
                up(g, 1)
                if h == 0:
                    ranks(0)
                if h == 1:
                    slot_tokens(1, 0, BATCHES // 2)
                up(g, 2)
                if h == 1:
                    slot_tokens(1, BATCHES // 2, BATCHES)
                down(g, 0)
                if h == 0:
                    down(g, 1)
                    up(g, 3)
                    slot_tokens(0, 0, BATCHES)
                else:
                    up(g, 3)
                    down(g, 1)
                down(g, 2)
                if ahead is not None:
                    logits(ahead, ahead)
                    to_rows(ahead, 0)
                down(g, 3)
                if ahead is not None and ahead < HG - 1:
                    to_rows(ahead, 1)

            def experts(h):
                weights_of = {}

                def to_channels(S, s, k, i):
                    pe.wait_ge(s_xg[k % XR], 2 * 16 * (STEPS // XR * h + turns(k, i, XR) + 1))
                    after(pe, s_exlo, S - 1)
                    for u in range(2):
                        for c in range(CC):
                            last = nc.tensor.transpose(ps_x[k % 2][:, c * 2 * P + u * P:c * 2 * P + (u + 1) * P],
                                                       xg[:, k % XR, u, c * P:(c + 1) * P], ident[:, :])
                    last.then_inc(s_ext, 1)

                def load_experts(s):
                    _, loaded = nc.values_load_multi_w_load_instructions(
                        exp_i[h][0:1, 2 * s:2 * s + 4], engines=[mybir.EngineType.PE],
                        min_val=0, max_val=(E - 1) * CHUNK)
                    for n in range(4):
                        weights_of[2 * s + n] = loaded[n]
                        weights_of.pop(2 * (s - 5) + n, None)

                def products(bank, hi, lo, s, first):
                    for u in range(2):
                        e = weights_of[2 * s + u]
                        for c in range(CC):
                            col = e + (EXP + first + c * C)
                            last = three(bank[:, u * C:(u + 1) * C], hi[:, c, u * P:(u + 1) * P],
                                         lo[:, c, u * P:(u + 1) * P], w_hi[:, bass.ds(col, C)],
                                         w_lo[:, bass.ds(col, C)], c == 0, c == CC - 1)
                    return last

                def step(s, k, i):
                    S = STEPS * h + s
                    if s % 2 == 0 and 0 < s < STEPS:
                        load_experts(s)
                    if s == 1:
                        pe.wait_ge(s_base, 2 * (HG + h))
                    if k < STEPS:
                        to_channels(S, s, k, i)
                    if h == 0 and i is not None and k == PEEL + 2:
                        to_rows(HG + i, 0)
                    if 1 <= k <= STEPS:
                        pe.wait_ge(s_exlo, S)
                        after(pe, s_ege, S - 1)
                        products(ps[1], xt_hi[(k - 1) % 2], xt_lo[(k - 1) % 2], s - 1, 0).then_inc(s_eup, 1)
                    if 2 <= k <= STEPS + 1:
                        pe.wait_ge(s_ege, S - 1)
                        after(pe, s_ehlo, S - 3)
                        for u in range(2):
                            for m in range(CC):
                                last = nc.tensor.transpose(ps_h[k % 2][:, m * 2 * P + u * P:m * 2 * P + (u + 1) * P],
                                                           gelu[:, k % 2, u * C + m * P:u * C + (m + 1) * P],
                                                           ident[:, :])
                        last.then_inc(s_eht, 1)
                    if k == STEPS + 2:
                        pe.wait_ge(s_xlo, HG + h + 1)
                        pe.wait_ge(s_ege, STEPS * (h + 1))
                        up(HG + h, 0)
                    if 3 <= k:
                        pe.wait_ge(s_ehlo, S - 2)
                        after(pe, s_ey, S - 3)
                        products(ps[3], ht_hi[(k - 3) % 2], ht_lo[(k - 3) % 2], s - 3, CC * C).then_inc(s_edn, 1)
                    if h == 0 and i is not None and k == PEEL + 1:
                        logits(HG + i, i)
                    if h == 0 and i is not None and k == PEEL + 2:
                        to_rows(HG + i, 1)
                    if h == 0 and k == STEPS + 1:
                        ranks(1)

                pe.wait_ge(s_place, h * PLACE_STEPS + EXPERT_STEP)
                load_experts(0)
                pe.wait_ge(s_wlo, NCHUNK)
                pe.wait_ge(s_hid, (HG + h) * SB)
                expert_phase(nc.tensor.Fori, step)

            pe.wait_ge(s_const, 9)
            pe.wait_ge(s_front, FRONT_STEPS)
            to_rows(0, 0)
            to_rows(0, 1)
            cond_products()
            for g in range(HG - 1):
                shared(g, g + 1)
            shared(HG - 1, None, 0)
            experts(0)
            pe.wait_ge(s_ey, STEPS)
            shared(HG, None, 1)
            experts(1)
            pe.wait_ge(s_ey, 2 * STEPS)
            for g in range(HG + 1, NG):
                shared(g)


def kernel(**inputs):
    import numpy as np
    import concourse.bacc as bacc
    from concourse.bass_utils import run_bass_kernel_spmd

    f = {k: np.asarray(v) for k, v in inputs.items()}
    x = f["x"]
    B, seq, C = x.shape
    CC = C // P
    N = B * seq
    w1, w3, w2 = f["L1_cond_w1"], f["L1_cond_w3"], f["L1_cond_w2"]
    w1e, w2e = f["L1_cond_W1e"], f["L1_cond_W2e"]
    E = w1e.shape[0]

    cols = []
    for b in range(w1.shape[1] // P):
        for w in (w1, w3):
            for c in range(CC):
                cols.append(w[c * P:(c + 1) * P, b * P:(b + 1) * P])
    for b in range(w2.shape[0] // P):
        cols.append(w2[b * P:(b + 1) * P, :])
    for e in range(E):
        for w in (w1e[e], w2e[e]):
            for c in range(CC):
                cols.append(w[c * P:(c + 1) * P, :])
    arrays = {
        "x_t": np.ascontiguousarray(x.transpose(2, 0, 1).reshape(CC, P, N)),
        "cond_t": np.ascontiguousarray(f["cond_1024"].T.reshape(CC, P, B).transpose(1, 0, 2)),
        "router_w": np.ascontiguousarray(f["L1_cond_router_W"].reshape(2 * CC, P, E).transpose(1, 0, 2)),
        "router_b": np.ascontiguousarray(f["L1_cond_router_bias"]),
        "w_all": np.ascontiguousarray(np.concatenate(cols, axis=1)),
    }
    nc = bacc.Bacc("TRN2", target_bir_lowering=False, num_devices=1)
    F32 = mybir.dt.float32
    aps = [nc.dram_tensor(n, a.shape, mybir.dt.from_np(a.dtype), kind="ExternalInput").ap() for n, a in arrays.items()]
    out = nc.dram_tensor("out", (N, C), F32, kind="ExternalOutput").ap()
    x1_cols = nc.dram_tensor("x1_cols", (N // GT // HALVES, P, CC * GT), F32, kind="Internal").ap()
    x1_rows = [nc.dram_tensor(f"x1_rows{h}", (N // HALVES, C), F32, kind="Internal").ap() for h in range(HALVES)]
    slots = expert_tiles(N // HALVES, E) * P
    y_rows = [nc.dram_tensor(f"y_rows{h}", (slots, C), F32, kind="Internal").ap() for h in range(HALVES)]
    build_spiking_moe(nc, *aps, out, x1_cols, x1_rows, y_rows)
    r = run_bass_kernel_spmd(nc, [arrays], core_ids=[0])
    return r.results[0]["out"].reshape(B, seq, C)
```

```python
import concourse.bass as bass
from concourse import mybir
from contextlib import ExitStack

P = 128
T = 256
GT = 512
HALVES = 2
CHUNK = 1024


def expert_tiles(tokens, experts):
    tiles = 2 * tokens // P + experts - 1
    return tiles + tiles % 2


def build_spiking_moe(nc, x_t, cond_t, router_w, router_b, w_all, out, x1_cols, x1_rows, y_rows):
    F32 = mybir.dt.float32
    F32R = mybir.dt.float32r
    I32 = mybir.dt.int32
    U32 = mybir.dt.uint32
    ALU = mybir.AluOpType
    ACT = mybir.ActivationFunctionType
    AX = mybir.AxisListType

    CC, _, N = x_t.shape
    C = CC * P
    NB = cond_t.shape[2]
    E = router_b.shape[0]
    NG = N // GT
    HG = NG // HALVES
    BG = GT // T
    TT = GT // P
    NT = N // P
    HT = NT // HALVES
    SB = 4
    UP_S, DN_S, EXP = 0, 2 * CHUNK, 3 * CHUNK
    SHARED_CHUNKS = EXP // CHUNK
    NCHUNK = SHARED_CHUNKS + E
    TILES = expert_tiles(N // HALVES, E)
    STEPS = TILES // 2
    XR = 4
    TURNS = STEPS // XR - 1
    assert (TURNS + 1) * XR == STEPS and TURNS == HG
    UNITS = NT // 2
    DT = 0.001
    PER_SPIKE = 999.99993896484375
    THIRD = 1.0 / 3.0
    PS_COND = 2 * HT * E
    YR = 4
    HOTS = 8
    BATCHES = 2 * HT // HOTS
    INST = 2 * HT

    ctx = ExitStack()
    with ctx:
        def sb(name, shape, dt=F32):
            return ctx.enter_context(nc.sbuf_tensor(name, shape, dt))

        def sem(name):
            return ctx.enter_context(nc.semaphore(name))

        w_hi = sb("w_hi", [P, NCHUNK * CHUNK], F32R)
        w_lo = sb("w_lo", [P, NCHUNK * CHUNK], F32R)
        base = sb("base", [P, NT, C])
        w_raw_s = base[:, NT - 4 * SHARED_CHUNKS:NT, :].rearrange("p (k t) c -> p k (t c)", k=SHARED_CHUNKS)
        xg = sb("xg", [P, XR, 2, C])
        w_raw_e = xg[:, :, :, :].rearrange("p (k r) u c -> p k (r u c)", k=2)
        rw = sb("rw", [P, 2 * CC, E])
        rb = sb("rb", [P, E])
        cond = sb("cond", [P, CC, NB])
        cond_rw = sb("cond_rw", [P, CC, NB, E])
        cond_logit = sb("cond_logit", [P, NB, E])
        ones = sb("ones", [P, T])
        ident = sb("ident", [P, P])
        earlier = sb("earlier", [P, P])
        count = sb("count", [P, P])
        same_e = sb("same_e", [P, E, HT])
        tok = sb("tok", [P, 2, HT])
        x_in = sb("x_in", [P, CC, BG, T])
        init = sb("init", [P, CC, BG])
        x1 = sb("x1", [P, CC, GT])
        front = sb("front", [P, 4, BG * (T + 1) + 2])
        W1 = BG * (T + 1)
        yv = [front[:, 2 * n:2 * n + 2, :].rearrange("p a b -> p (a b)")[:, 0:4 * C].rearrange(
            "p (q c) -> p q c", q=4) for n in range(2)]
        yv.append(x_in[:, :, :, :].rearrange("p c b t -> p (c b) t"))
        yv.append(x1[:, :, :].rearrange("p c n -> p (c n)").rearrange("p (q c) -> p q c", q=4))
        logit = sb("logit", [P, HT, E])
        score = sb("score", [P, HT, E])
        sel = logit
        top = sb("top", [P, HT, 8])
        top_i = sb("top_i", [P, HT, 8], U32)
        top_f = sb("top_f", [P, 2, HT])
        hot_s = sb("hot_s", [P, 2, HT, E])
        chosen = sb("chosen", [P, 2, HT])
        denom = sb("denom", [P, HT])
        denom_e = sb("denom_e", [P, HT])
        recip = sb("recip", [P, HT])
        big = sb("big", [P, HT])
        half = sb("half", [P, HT])
        recip_g = sb("recip_g", [P, HT])
        gate_m = sb("gate_m", [P, 2, HT])
        gate = sb("gate", [P, 2, NT])
        hot = sb("hot", [P, 2, HT, E])
        member = sb("member", [P, E, HT])
        prefix = sb("prefix", [P, E, HT])
        prefix_x = sb("prefix_x", [P, E, HT])
        n127 = sb("n127", [P, E], I32)
        n_tiles_i = sb("n_tiles_i", [P, E], I32)
        n_tiles = sb("n_tiles", [P, E])
        end_tile = sb("end_tile", [P, E])
        first_tile = sb("first_tile", [P, E])
        first_slot = sb("first_slot", [P, E])
        slot_e = prefix_x
        slot_f = sb("slot_f", [P, INST])
        slot_i = [sb(f"slot_i{h}", [P, INST], I32) for h in range(HALVES)]
        lane_i = sb("lane_i", [P, INST], I32)
        tile_i = sb("tile_i", [P, INST], I32)
        lane_f = sb("lane_f", [P, INST])
        tile_f = sb("tile_f", [P, INST])
        lane_hot = sb("lane_hot", [P, 2, HOTS, P], F32R)
        tile_hot = sb("tile_hot", [P, INST, TILES], F32R)
        tok_i = sb("tok_i", [P, TILES], I32)
        past_e = sb("past_e", [1, TILES, E])
        exp_f = sb("exp_f", [1, TILES])
        exp_i = [sb(f"exp_i{h}", [1, TILES], I32) for h in range(HALVES)]
        g_col = sb("g_col", [P, 2, 4], I32)
        c_col = sb("c_col", [P, YR, 4], I32)
        x_re = sb("x_re", [P, CC, GT])
        x_hi = sb("x_hi", [P, CC, GT], F32R)
        x_lo = sb("x_lo", [P, CC, GT], F32R)
        parts = sb("parts", [P, 8, GT], F32R)
        hid_hi, hid_lo = parts[:, 0:SB, :], parts[:, SB:2 * SB, :]
        xt_hi = [parts[:, n, :].rearrange("p (c s) -> p c s", c=CC) for n in (0, 1)]
        xt_lo = [parts[:, n, :].rearrange("p (c s) -> p c s", c=CC) for n in (2, 3)]
        ht_hi = [parts[:, n, :].rearrange("p (c s) -> p c s", c=CC) for n in (4, 5)]
        ht_lo = [parts[:, n, :].rearrange("p (c s) -> p c s", c=CC) for n in (6, 7)]
        works = sb("works", [P, 4, GT])
        act, hid = works[:, 0:2, :], works[:, 2:4, :]
        gelu, y_sb = works[:, 0:2, :], works[:, 2:4, :]

        def front_views(rows):
            short = [r[:, 0:BG * T].rearrange("p (b t) -> p b t", b=BG) for r in rows]
            full = [r[:, 0:W1].rearrange("p (b t) -> p b t", b=BG) for r in rows]
            return short[0], full[0], short[1], full[1], full[2], short[2], full[3].bitcast(I32)

        front_main = front_views([front[:, n, :] for n in range(4)])
        works_flat = works[:, :, :].rearrange("p a n -> p (a n)")
        front_side = front_views([works_flat[:, n * W1:(n + 1) * W1] for n in range(3)]
                                 + [x_re[:, :, :].rearrange("p c n -> p (c n)")])

        def front_of(g, c):
            return front_side if (g, c) == (0, 1) else front_main

        ps = [ctx.enter_context(nc.psum_tensor(f"ps{n}", [P, GT], F32)) for n in range(4)]
        ps_d = [ctx.enter_context(nc.psum_tensor(f"ps_d{n}", [P, GT], F32)) for n in range(2)]
        ps_x, ps_h = [ps[0], ps_d[0]], [ps[2], ps_d[1]]
        ps_r = ctx.enter_context(nc.psum_tensor("ps_r", [P, GT], F32))
        ps_t = ctx.enter_context(nc.psum_tensor("ps_t", [P, GT], F32))

        s_w = [sem(f"w_loaded{n}") for n in range(NCHUNK)]
        s_small = sem("small_loaded")
        s_const = sem("const_made")
        s_whi = sem("w_hi_made")
        s_wlo = sem("w_lo_made")
        s_crw = sem("cond_rw_made")
        s_cl = sem("cond_logit_summed")
        s_clc = sem("cond_logit_kept")
        s_x = [sem(f"x_loaded{c}") for c in range(CC)]
        s_front = sem("front_step")
        s_logit = sem("logits_summed")
        s_score = sem("scores_made")
        s_xt = sem("x1_transposed")
        s_xev = sem("x1_rows_copied")
        s_xrow = [sem(f"x1_rows_stored{n}") for n in range(HG + 1)]
        s_xst = sem("x1_cols_stored")
        s_xre = sem("x1_cols_reloaded")
        s_xhi = sem("x_hi_made")
        s_xlo = sem("x_lo_made")
        s_part = sem("first_x_parts_made")
        s_place = sem("place_step")
        s_ranks = sem("ranks_summed")
        s_rate = sem("rates_made")
        s_int = sem("potentials_rounded")
        s_hot = sem("lane_one_hots_made")
        s_thot = sem("tile_one_hots_made")
        s_used = sem("one_hots_used")
        s_up = sem("up_done")
        s_act = sem("silu_made")
        s_hid = sem("hidden_made")
        s_hhi = sem("hid_hi_made")
        s_hlo = sem("hid_lo_made")
        s_down = sem("down_done")
        s_base = sem("base_made")
        s_xg = [sem(f"rows_gathered{n}") for n in range(XR)]
        s_gcol = sem("gather_columns_copied")
        s_ext = sem("exp_x_transposed")
        s_exhi = sem("exp_x_hi_made")
        s_exlo = sem("exp_x_lo_made")
        s_eup = sem("exp_up_done")
        s_ege = sem("exp_gelu_made")
        s_eht = sem("exp_h_transposed")
        s_ehhi = sem("exp_h_hi_made")
        s_ehlo = sem("exp_h_lo_made")
        s_edn = sem("exp_down_done")
        s_ey = sem("exp_y_copied")
        s_yst = [sem(f"y_stored{n}") for n in range(2)]
        s_ccol = sem("sum_columns_copied")
        s_yv = [sem(f"y_gathered{n}") for n in range(YR)]
        s_cmid = sem("first_choice_added")
        s_comb = sem("unit_summed")
        s_out = sem("out_stored")

        FRONT_STEPS = 18
        LOGIT_STEP, PREFIX_STEP = 1, 8 + 2 * HT
        TILE_STEP, TOKEN_STEP, EXPERT_STEP, PLACE_STEPS = 25 + 2 * HT, 26 + 2 * HT, 29 + 2 * HT, 40 + 2 * HT

        def after(engine, semaphore, value):
            if value > 0:
                engine.wait_ge(semaphore, value)

        def front_count(g, c, k):
            if g == 0:
                return 5 * c + k if k <= 5 else 2 * k - 1 + c
            return g * FRONT_STEPS + c * FRONT_STEPS // CC + k

        def rows_stored(engine, h, g):
            engine.wait_ge(s_xrow[HG if h == 1 else g], 16 * HG if h == 1 else 16)

        def turn_of(h, s):
            return s // XR - 1 if h == 0 and XR <= s < STEPS else None

        def front_beside(s):
            return HG + s // XR if s < STEPS - XR else None

        def unit_beside(s):
            return s // 3 + 1 if s >= 3 and s % 3 == 0 and s // 3 + 1 < UNITS // 2 else None

        block = ctx.enter_context(nc.Block())

        @block.sync
        def _(sp):
            def load_x(g, c):
                if g > 0:
                    sp.wait_ge(s_front, front_count(g - 1, c, FRONT_STEPS // CC))
                sp.dma_start(x_in[:, c, :, :].rearrange("p b t -> p (b t)"),
                             x_t[c, :, bass.ds(g * GT, GT)]).then_inc(s_x[c], 16)
                sp.dma_start(init[:, c, :], cond_t[:, c, bass.ds(g * BG, BG)]).then_inc(s_x[c], 16)

            def store_cols(g):
                sp.wait_ge(s_front, (g + 1) * FRONT_STEPS)
                sp.dma_start(x1_cols[bass.ds(g - HG, 1), :, :].rearrange("a p n -> p (a n)"),
                             x1[:, :, :].rearrange("p c n -> p (c n)")).then_inc(s_xst, 16)

            def store_rows(g, h):
                sp.wait_ge(s_xev, 2 * (g + 1))
                sp.dma_start(x1_rows[h][bass.ds((g - h * HG) * GT, GT), :].rearrange("(t p) c -> p t c", p=P),
                             base[:, bass.ds(g * TT, TT), :]).then_inc(s_xrow[HG if h == 1 else g], 16)

            def reload(g):
                sp.wait_ge(s_xst, 16 * (g - HG + 1))
                after(sp, s_xlo, g)
                sp.dma_start(x_re[:, :, :].rearrange("p c n -> p (c n)"),
                             x1_cols[bass.ds(g - HG, 1), :, :].rearrange("a p n -> p (a n)")).then_inc(s_xre, 16)

            def store_y(h, s):
                sp.wait_ge(s_ey, STEPS * h + s + 1)
                sp.dma_start(y_rows[h][bass.ds(s * 2 * P, 2 * P), :].rearrange("(u p) c -> p u c", p=P),
                             y_sb[:, s % 2, :].rearrange("p (u c) -> p u c", u=2)).then_inc(s_yst[s % 2], 16)

            def experts(h):
                for s in range(STEPS + 3):
                    i = turn_of(h, s)
                    if i is not None and s % XR == 0 and front_beside(s) is not None:
                        load_x(HG + 1 + i, 0)
                    if i is not None and s % XR == 1:
                        store_cols(HG + i)
                        if front_beside(s) is not None:
                            load_x(HG + 1 + i, 1)
                        else:
                            reload(HG)
                    if 3 <= s:
                        store_y(h, s - 3)
                    if i is not None and s % XR == 3:
                        store_rows(HG + i, 1)
                    if h == 1 and (s < 2 or unit_beside(s - 2) is not None):
                        store_out(s if s < 2 else unit_beside(s - 2))

            def store_out(u):
                sp.wait_ge(s_comb, u + 1)
                sp.wait_ge(s_base, u + 1)
                sp.dma_start(out[bass.ds(u * 2 * P, 2 * P), :].rearrange("(t p) c -> p t c", p=P),
                             base[:, bass.ds(u * 2, 2), :]).then_inc(s_out, 16)

            load_x(0, 0)
            sp.dma_start(rw[:, :, :], router_w).then_inc(s_small, 16)
            sp.dma_start(cond[:, :, :], cond_t).then_inc(s_small, 16)
            sp.dma_start(rb[:, :], router_b.partition_broadcast(P)).then_inc(s_small, 16)
            load_x(0, 1)
            for k in range(SHARED_CHUNKS):
                sp.dma_start(w_raw_s[:, k, :], w_all[:, k * CHUNK:(k + 1) * CHUNK]).then_inc(s_w[k], 16)
            load_x(1, 0)
            load_x(1, 1)
            for g in range(HG):
                store_rows(g, 0)
                if g + 2 <= HG:
                    load_x(g + 2, 0)
                    load_x(g + 2, 1)
            experts(0)
            reload(HG + 1)
            reload(HG + 2)
            experts(1)
            reload(HG + 3)
            for u in range(UNITS // 2, UNITS):
                store_out(u)
            sp.wait_ge(s_out, 16 * UNITS)

        @block.gpsimd
        def _(pool):
            def load_w(k):
                if k >= SHARED_CHUNKS + 2:
                    pool.wait_ge(s_wlo, k - 1)
                nc.gpsimd.dma_start(w_raw_e[:, k % 2, :], w_all[:, k * CHUNK:(k + 1) * CHUNK]).then_inc(s_w[k], 16)

            nc.gpsimd.memset(ones[:, :], 1.0).then_inc(s_const, 1)
            nc.gpsimd.memset(ident[:, :], 0.0).then_inc(s_const, 1)
            nc.gpsimd.memset(earlier[:, :], 1.0).then_inc(s_const, 1)
            nc.gpsimd.memset(same_e[:, :, :], 1.0).then_inc(s_const, 1)
            nc.gpsimd.iota(count[:, :], pattern=[[1, P]], base=0, channel_multiplier=0,
                           allow_small_or_imprecise_dtypes=True).then_inc(s_const, 1)
            nc.gpsimd.iota(tok[:, :, :], pattern=[[0, 2], [P, HT]], base=0, channel_multiplier=1,
                           allow_small_or_imprecise_dtypes=True).then_inc(s_const, 1)
            pool.wait_ge(s_const, 6)
            nc.gpsimd.affine_select(out=ident[:, :], in_=ident[:, :], compare_op=ALU.not_equal, fill=1.0,
                                    base=0, pattern=[[-1, P]], channel_multiplier=1).then_inc(s_const, 1)
            nc.gpsimd.affine_select(out=earlier[:, :], in_=earlier[:, :], compare_op=ALU.is_gt, fill=0.0,
                                    base=0, pattern=[[1, P]], channel_multiplier=-1).then_inc(s_const, 1)
            nc.gpsimd.memset(same_e[:, :, 0:1], 0.0).then_inc(s_const, 1)
            for k in range(NCHUNK):
                cols = slice(k * CHUNK, (k + 1) * CHUNK)
                raw = w_raw_s[:, k, :] if k < SHARED_CHUNKS else w_raw_e[:, k % 2, :]
                pool.wait_ge(s_w[k], 16)
                pool.wait_ge(s_whi, k + 1)
                nc.gpsimd.tensor_tensor(w_lo[:, cols], raw, w_hi[:, cols].bitcast(F32), ALU.subtract).then_inc(s_wlo, 1)
                if SHARED_CHUNKS <= k < NCHUNK - 2:
                    load_w(k + 2)
                if k == 0:
                    load_w(SHARED_CHUNKS)
                    load_w(SHARED_CHUNKS + 1)

            def gather(h, s):
                if s % 2 == 0:
                    for r in range(2):
                        after(pool, s_xg[s % XR + r], 2 * 16 * (STEPS // XR * h + s // XR))
                    nc.gpsimd.tensor_copy(g_col[:, s // 2 % 2, :], tok_i[:, bass.ds(2 * s, 4)]).then_inc(s_gcol, 1)
                    pool.wait_ge(s_gcol, STEPS // 2 * h + s // 2 + 1)
                after(pool, s_ext, STEPS * h + s - XR + 1)
                for u in range(2):
                    c = 2 * (s % 2) + u
                    nc.gpsimd.indirect_dma_start(
                        xg[:, s % XR, u, :], None, x1_rows[h],
                        bass.IndirectOffsetOnAxis(ap=g_col[:, s // 2 % 2, c:c + 1], axis=0)).then_inc(s_xg[s % XR], 16)

            def gather_y(h, u):
                par = u % YR
                after(pool, s_comb, u - YR + 1)
                nc.gpsimd.tensor_copy(c_col[:, par, :].rearrange("p (t k) -> p k t", k=2),
                                      slot_i[h][:, :].rearrange("p (k t) -> p k t", k=2)[:, :, bass.ds(2 * u - h * HT, 2)]
                                      ).then_inc(s_ccol, 1)
                pool.wait_ge(s_ccol, u + 1)
                for q in range(4):
                    nc.gpsimd.indirect_dma_start(
                        yv[par][:, q, :], None, y_rows[h],
                        bass.IndirectOffsetOnAxis(ap=c_col[:, par, q:q + 1], axis=0)).then_inc(s_yv[par], 16)

            def tile_hots(h):
                pool.wait_ge(s_place, h * PLACE_STEPS + TILE_STEP - 1)
                nc.gpsimd.tensor_tensor(tile_hot[:, HT:, :], tile_hot[:, HT:, :].bitcast(F32),
                                        tok[:, 1, :].unsqueeze(2).to_broadcast([P, HT, TILES]), ALU.mult).then_inc(s_thot, 1)

            def y_rows_stored(h):
                for n in range(2):
                    pool.wait_ge(s_yst[n], 16 * (h + 1) * STEPS // 2)

            def experts(h):
                pool.wait_ge(s_place, h * PLACE_STEPS + TOKEN_STEP)
                for g in range(HG):
                    rows_stored(pool, h, g)
                for s in range(STEPS):
                    gather(h, s)
                    if h == 1 and unit_beside(s) is not None:
                        gather_y(0, unit_beside(s))

            pool.wait_ge(s_wlo, NCHUNK)
            tile_hots(0)
            experts(0)
            tile_hots(1)
            y_rows_stored(0)
            pool.wait_ge(s_front, NG * FRONT_STEPS)
            pool.wait_ge(s_logit, NG)
            pool.wait_ge(s_xt, 2 * NG)
            pool.wait_ge(s_xst, 16 * HG)
            gather_y(0, 0)
            gather_y(0, 1)
            experts(1)
            y_rows_stored(1)
            for u in range(UNITS // 2, UNITS):
                gather_y(1, u)

        @block.scalar
        def _(act_e):
            def split(g, half):
                if half == 0:
                    act_e.wait_ge(s_front, (g + 1) * FRONT_STEPS)
                else:
                    act_e.wait_ge(s_xre, 16 * (g - HG + 1))
                after(act_e, s_up, g * SB)
                after(act_e, s_xlo, g)
                nc.scalar.activation(x_hi[:, :, :], (x1 if half == 0 else x_re)[:, :, :], ACT.Copy).then_inc(s_xhi, 1)

            def split_first():
                for c in range(CC):
                    act_e.wait_ge(s_front, front_count(0, c, FRONT_STEPS // CC))
                    nc.scalar.activation(x_hi[:, c, :], x1[:, c, :], ACT.Copy).then_inc(
                        s_xhi if c == CC - 1 else s_part, 1)

            def copy_rows(g, r):
                act_e.wait_ge(s_xt, 2 * g + r + 1)
                nc.scalar.activation(base[:, bass.ds(g * TT + 2 * r, 2), :].rearrange("p t c -> p (t c)"),
                                     ps_t[:, :], ACT.Copy).then_inc(s_xev, 1)

            def split_w(k):
                act_e.wait_ge(s_w[k], 16)
                raw = w_raw_s[:, k, :] if k < SHARED_CHUNKS else w_raw_e[:, k % 2, :]
                nc.scalar.activation(w_hi[:, k * CHUNK:(k + 1) * CHUNK], raw, ACT.Copy).then_inc(s_whi, 1)

            def scores(h):
                act_e.wait_ge(s_place, h * PLACE_STEPS + LOGIT_STEP)
                nc.scalar.activation(score[:, :, :], logit[:, :, :], ACT.Sigmoid).then_inc(s_score, 1)

            def rates_of(g, c):
                act_e.wait_ge(s_x[c], 32 * (g + 1))
                if g > 0:
                    act_e.wait_ge(s_front, front_count(g, c, 0) - 1)
                nc.scalar.activation(front_of(g, c)[0], x_in[:, c, :, :], ACT.Relu, scale=DT).then_inc(s_rate, 1)

            def rounded(g, c):
                act_e.wait_ge(s_front, front_count(g, c, 5))
                pot, pot_int = front_of(g, c)[4], front_of(g, c)[6]
                nc.scalar.activation(pot_int, pot, ACT.Copy).then_inc(s_int, 1)

            def silu(g, b):
                act_e.wait_ge(s_up, g * SB + b + 1)
                after(act_e, s_hid, g * SB + b - 1)
                nc.scalar.activation(act[:, b % 2, :], ps[2 * (b % 2)][:, :], ACT.Silu).then_inc(s_act, 1)

            def shared(g, ahead):
                if 0 < g and g + 1 < HG:
                    rounded(g + 1, 1)
                for b in range(SB):
                    if (g, b) != (0, 1) and (b > 0 or g not in (0, HG - 1, HG, HG + 1)):
                        silu(g, b)
                    if g + 2 < HG and b == 2:
                        rounded(g + 2, 0)
                    act_e.wait_ge(s_hid, g * SB + b + 1)
                    after(act_e, s_down, g * SB + b + 1 - SB)
                    nc.scalar.activation(hid_hi[:, b, :], hid[:, b % 2, :], ACT.Copy).then_inc(s_hhi, 1)
                    if g == 0 and b == 0:
                        silu(0, 1)
                        rounded(1, 1)
                    if g + 2 < HG and b == 1:
                        rates_of(g + 2, 0)
                    if g < HG - 1 and b < 3 and SHARED_CHUNKS + 3 * g + b < NCHUNK:
                        split_w(SHARED_CHUNKS + 3 * g + b)
                if ahead is not None:
                    split(ahead, ahead // HG)
                    if ahead == HG - 1:
                        scores(0)
                    if g + 2 < HG:
                        rates_of(g + 2, 1)
                    if ahead < HG:
                        copy_rows(ahead, 0)
                        if ahead == HG - 1:
                            silu(ahead, 0)
                        copy_rows(ahead, 1)

            def experts(h):
                for s in range(STEPS + 3):
                    i = turn_of(h, s)
                    S = STEPS * h + s
                    if h == 0 and s == STEPS + 1:
                        split(HG, 1)
                    if s < STEPS:
                        act_e.wait_ge(s_ext, S + 1)
                        after(act_e, s_eup, S - 1)
                        nc.scalar.activation(xt_hi[s % 2].rearrange("p c s -> p (c s)"), ps_x[s % 2][:, :],
                                             ACT.Copy).then_inc(s_exhi, 1)
                    if i is not None and s % XR >= 2:
                        copy_rows(HG + i, s % XR - 2)
                    if 1 <= s <= STEPS:
                        act_e.wait_ge(s_eup, S)
                        after(act_e, s_eht, S - 2)
                        nc.scalar.activation(gelu[:, (s - 1) % 2, :], ps[1][:, :], ACT.Gelu).then_inc(s_ege, 1)
                    if i is not None and s % XR == 0:
                        rounded(HG + i, 1)
                    elif h == 0 and s % XR and front_beside(s) is not None:
                        if s % XR == 2:
                            rounded(front_beside(s), 0)
                        else:
                            rates_of(front_beside(s), s % XR // 2)
                    if 2 <= s <= STEPS + 1:
                        act_e.wait_ge(s_eht, S - 1)
                        after(act_e, s_edn, S - 3)
                        nc.scalar.activation(ht_hi[s % 2].rearrange("p c s -> p (c s)"), ps_h[s % 2][:, :],
                                             ACT.Copy).then_inc(s_ehhi, 1)
                    if s == STEPS + 2:
                        silu(HG + h, 0)
                    if 3 <= s:
                        act_e.wait_ge(s_edn, S - 2)
                        after(act_e, s_yst[(s - 3) % 2], 16 * (STEPS // 2 * h + (s - 3) // 2))
                        nc.scalar.activation(y_sb[:, (s - 3) % 2, :], ps[3][:, :], ACT.Copy).then_inc(s_ey, 1)
                    if i == TURNS - 1 and s % XR == 2:
                        scores(1)

            rates_of(0, 0)
            rates_of(0, 1)
            rounded(0, 0)
            rounded(0, 1)
            split_w(0)
            split_first()
            split_w(1)
            split_w(2)
            copy_rows(0, 0)
            rates_of(1, 0)
            rounded(1, 0)
            silu(0, 0)
            copy_rows(0, 1)
            act_e.wait_ge(s_cl, 1)
            nc.scalar.activation(cond_logit[:, :, :].rearrange("p b e -> p (b e)"), ps_r[:, PS_COND:PS_COND + NB * E],
                                 ACT.Copy).then_inc(s_clc, 1)
            rates_of(1, 1)
            for g in range(HG - 1):
                shared(g, g + 1)
            shared(HG - 1, None)
            act_e.wait_ge(s_down, HG * SB)
            act_e.wait_ge(s_hlo, HG * SB)
            act_e.wait_ge(s_wlo, SHARED_CHUNKS)
            experts(0)
            act_e.wait_ge(s_eht, STEPS)
            shared(HG, HG + 1)
            act_e.wait_ge(s_down, (HG + 1) * SB)
            act_e.wait_ge(s_hlo, (HG + 1) * SB)
            experts(1)
            act_e.wait_ge(s_eht, 2 * STEPS)
            shared(HG + 1, HG + 2)
            shared(HG + 2, HG + 3)
            shared(HG + 3, None)

        @block.vector
        def _(dve):
            def front_steps(g):
                n = FRONT_STEPS // CC

                def done(ins):
                    ins.then_inc(s_front, 1)

                def chunk(c):
                    rates, floors, sums, above, pot, spikes, pot_int = front_of(g, c)

                    def need(k):
                        dve.wait_ge(s_front, front_count(g, c, k))

                    def start_col():
                        if g > 0:
                            dve.wait_ge(s_front, front_count(g, c, 0))
                        dve.wait_ge(s_x[c], 32 * (g + 1))
                        done(nc.vector.tensor_scalar(pot[:, :, 0], init[:, c, :], 0.0, None, ALU.add))

                    def scan(b):
                        dve.wait_ge(s_rate, CC * g + c + 1)
                        done(nc.vector.tensor_tensor_scan(sums[:, b, :], ones[:, :], rates[:, b, :], 0.0,
                                                          ALU.mult, ALU.add))

                    def add_init(b):
                        need(2 + b)
                        done(nc.vector.tensor_scalar(pot[:, b, 1:T + 1], sums[:, b, :], init[:, c, b:b + 1],
                                                     None, ALU.add))

                    def rounded_up():
                        dve.wait_ge(s_int, CC * g + c + 1)
                        done(nc.vector.tensor_tensor(above, pot_int, pot, ALU.is_gt))

                    def floor():
                        need(6)
                        done(nc.vector.tensor_tensor(floors, pot_int, above, ALU.subtract))

                    def spike():
                        need(7)
                        done(nc.vector.tensor_tensor(spikes, floors[:, :, 1:T + 1], floors[:, :, 0:T], ALU.subtract))

                    def new_x1():
                        need(8)
                        if c == 0:
                            after(dve, s_logit, g)
                            after(dve, s_xt, 2 * g)
                            if g <= HG:
                                after(dve, s_xhi, g)
                                after(dve, s_xlo, g)
                            else:
                                dve.wait_ge(s_xst, 16 * (g - HG))
                        done(nc.vector.scalar_tensor_tensor(
                            x1[:, c, :].rearrange("p (b t) -> p b t", b=BG), spikes,
                            PER_SPIKE, x_in[:, c, :, :], ALU.mult, ALU.add))

                    return [start_col, lambda: scan(0), lambda: scan(1), lambda: add_init(0),
                            lambda: add_init(1), rounded_up, floor, spike, new_x1]

                a, b = chunk(0), chunk(1)
                steps = a + b
                if g == 0:
                    steps = a[:5] + b[:5] + [f for pair in zip(a[5:], b[5:]) for f in pair]
                assert CC == 2 and len(a) == n and len(steps) == FRONT_STEPS
                return steps

            def place_steps(h):
                n = [0]
                base_n = h * PLACE_STEPS

                def done(ins):
                    n[0] += 1
                    ins.then_inc(s_place, 1)

                def need_last():
                    dve.wait_ge(s_place, base_n + n[0])

                def flat(t):
                    return t[:, :, :].rearrange("p a b -> p (a b)")

                def choose():
                    dve.wait_ge(s_logit, (h + 1) * HG)
                    done(nc.vector.tensor_tensor(
                        logit[:, :, :].rearrange("p (b t) e -> p b t e", t=T // P),
                        ps_r[:, 0:HT * E].rearrange("p (b t e) -> p b t e", t=T // P, e=E),
                        cond_logit[:, h * NB // HALVES:(h + 1) * NB // HALVES, :].unsqueeze(2)
                        .to_broadcast([P, NB // HALVES, T // P, E]), ALU.add))
                    assert n[0] == LOGIT_STEP

                def top_two():
                    dve.wait_ge(s_score, h + 1)
                    done(nc.vector.tensor_tensor(sel[:, :, :], score[:, :, :],
                                                 rb[:, :].unsqueeze(1).to_broadcast([P, HT, E]), ALU.add))
                    need_last()
                    for t in range(HT):
                        done(nc.vector.max(top[:, t, :], sel[:, t, :]))
                    need_last()
                    for t in range(HT):
                        done(nc.vector.max_index(top_i[:, t, :], top[:, t, :], sel[:, t, :]))
                    need_last()
                    done(nc.vector.tensor_copy(top_f[:, :, :].rearrange("p k t -> p t k"), top_i[:, :, 0:2]))
                    need_last()
                    for k in range(2):
                        done(nc.vector.tensor_tensor(hot[:, k, :, :],
                                                     count[:, 0:E].unsqueeze(1).to_broadcast([P, HT, E]),
                                                     top_f[:, k, :].unsqueeze(2).to_broadcast([P, HT, E]),
                                                     ALU.is_equal))
                    need_last()

                def prefixes():
                    done(nc.vector.tensor_tensor(member[:, :, :], hot[:, 0, :, :].rearrange("p t e -> p e t"),
                                                 hot[:, 1, :, :].rearrange("p t e -> p e t"), ALU.add))
                    need_last()
                    done(nc.vector.tensor_tensor_scan(flat(prefix), flat(same_e), flat(member), 0.0,
                                                      ALU.mult, ALU.add))
                    need_last()
                    done(nc.vector.tensor_tensor(prefix_x[:, :, :], prefix[:, :, :], member[:, :, :], ALU.subtract))
                    assert n[0] == PREFIX_STEP, n[0]

                def gates():
                    for k in range(2):
                        done(nc.vector.tensor_tensor(hot_s[:, k, :, :], hot[:, k, :, :], score[:, :, :], ALU.mult))
                    need_last()
                    done(nc.vector.tensor_reduce(chosen[:, :, :], hot_s[:, :, :, :], axis=AX.X, op=ALU.add))
                    need_last()
                    done(nc.vector.tensor_tensor(denom[:, :], chosen[:, 0, :], chosen[:, 1, :], ALU.add))
                    need_last()
                    done(nc.vector.tensor_scalar(denom_e[:, :], denom[:, :], 1e-9, None, ALU.add))
                    done(nc.vector.tensor_scalar(big[:, :], denom[:, :], 1e-9, None, ALU.is_gt))
                    need_last()
                    done(nc.vector.reciprocal(recip[:, :], denom_e[:, :]))
                    done(nc.vector.tensor_scalar(half[:, :], big[:, :], -0.5 * THIRD, 0.5 * THIRD, ALU.mult, ALU.add))
                    need_last()
                    done(nc.vector.scalar_tensor_tensor(recip_g[:, :], recip[:, :], THIRD, big[:, :],
                                                        ALU.mult, ALU.mult))
                    need_last()
                    done(nc.vector.tensor_tensor(gate_m[:, :, :], chosen[:, :, :],
                                                 recip_g[:, :].unsqueeze(1).to_broadcast([P, 2, HT]), ALU.mult))
                    need_last()
                    done(nc.vector.tensor_tensor(gate[:, :, h * HT:(h + 1) * HT], gate_m[:, :, :],
                                                 half[:, :].unsqueeze(1).to_broadcast([P, 2, HT]), ALU.add))
                    assert n[0] == PLACE_STEPS, n[0]

                def slots():
                    dve.wait_ge(s_ranks, h + 1)
                    done(nc.vector.tensor_scalar(n127[:, :], ps_r[:, 2 * HT * E:2 * HT * E + E], P - 1.0, None, ALU.add))
                    need_last()
                    done(nc.vector.tensor_scalar(n_tiles_i[:, :], n127[:, :], 7, None, ALU.logical_shift_right))
                    need_last()
                    done(nc.vector.tensor_copy(n_tiles[:, :], n_tiles_i[:, :]))
                    need_last()
                    done(nc.vector.tensor_tensor_scan(end_tile[:, :], ones[:, 0:E], n_tiles[:, :], 0.0,
                                                      ALU.mult, ALU.add))
                    need_last()
                    done(nc.vector.tensor_tensor(first_tile[:, :], end_tile[:, :], n_tiles[:, :], ALU.subtract))
                    need_last()
                    done(nc.vector.tensor_scalar(first_slot[:, :], first_tile[:, :], float(P), None, ALU.mult))
                    need_last()
                    done(nc.vector.tensor_tensor(slot_e[:, :, :],
                                                 ps_r[:, HT * E:2 * HT * E].rearrange("p (e t) -> p e t", e=E),
                                                 first_slot[:, :].unsqueeze(2).to_broadcast([P, E, HT]), ALU.add))
                    need_last()
                    for k in range(2):
                        done(nc.vector.tensor_tensor(hot_s[:, k, :, :], hot[:, k, :, :],
                                                     slot_e[:, :, :].rearrange("p e t -> p t e"), ALU.mult))
                    need_last()
                    done(nc.vector.tensor_reduce(slot_f[:, :].rearrange("p (k t) -> p k t", k=2), hot_s[:, :, :, :],
                                                 axis=AX.X, op=ALU.add))
                    need_last()
                    done(nc.vector.tensor_copy(slot_i[h][:, :], slot_f[:, :]))
                    need_last()
                    done(nc.vector.tensor_scalar(lane_i[:, :], slot_i[h][:, :], P - 1, None, ALU.bitwise_and))
                    done(nc.vector.tensor_scalar(tile_i[:, :], slot_i[h][:, :], 7, None, ALU.logical_shift_right))
                    need_last()
                    done(nc.vector.tensor_copy(lane_f[:, :], lane_i[:, :]))
                    done(nc.vector.tensor_copy(tile_f[:, :], tile_i[:, :]))
                    need_last()

                def tile_hots():
                    done(nc.vector.tensor_tensor(tile_hot[:, :, :], count[:, 0:TILES].unsqueeze(1).to_broadcast([P, INST, TILES]),
                                                 tile_f[:, :].unsqueeze(2).to_broadcast([P, INST, TILES]), ALU.is_equal))
                    need_last()
                    done(nc.vector.tensor_tensor(tile_hot[:, 0:HT, :], tile_hot[:, 0:HT, :].bitcast(F32),
                                                 tok[:, 0, :].unsqueeze(2).to_broadcast([P, HT, TILES]), ALU.mult))
                    assert n[0] == TILE_STEP, n[0]

                def lane_hots(b):
                    after(dve, s_used, h * BATCHES + b - 1)
                    nc.vector.tensor_tensor(lane_hot[:, b % 2, :, :], count[:, :].unsqueeze(1).to_broadcast([P, HOTS, P]),
                                            lane_f[:, b * HOTS:(b + 1) * HOTS].unsqueeze(2).to_broadcast([P, HOTS, P]),
                                            ALU.is_equal).then_inc(s_hot, 1)

                def tokens():
                    dve.wait_ge(s_used, (h + 1) * BATCHES)
                    after(dve, s_gcol, h * STEPS // 2)
                    done(nc.vector.tensor_copy(tok_i[:, :], ps_t[:, 0:TILES]))
                    assert n[0] == TOKEN_STEP, n[0]

                def tile_experts():
                    done(nc.vector.tensor_tensor(past_e[:, :, :], count[0:1, 0:TILES].unsqueeze(2).to_broadcast([1, TILES, E]),
                                                 end_tile[0:1, :].unsqueeze(1).to_broadcast([1, TILES, E]), ALU.is_ge))
                    need_last()
                    done(nc.vector.tensor_reduce(exp_f[:, :], past_e[:, :, :], axis=AX.X, op=ALU.add))
                    need_last()
                    done(nc.vector.tensor_scalar(exp_i[h][:, :], exp_f[:, :], E - 1.0, float(CHUNK),
                                                 ALU.min, ALU.mult))
                    assert n[0] == EXPERT_STEP, n[0]

                lanes = [lambda b=b: lane_hots(b) for b in range(BATCHES)]
                return [choose, top_two, prefixes, slots, tile_hots, *lanes, tokens, tile_experts, gates]

            def unit_steps(u, first=False):
                par, seen = u % YR, u // YR + 1
                def add(k):
                    if k == 0:
                        if first:
                            rows_stored(dve, 1, u // 2)
                        else:
                            dve.wait_ge(s_base, 2 * (u // 2 + 1))
                        dve.wait_ge(s_yv[par], 4 * 16 * seen)
                    else:
                        dve.wait_ge(s_cmid, u + 1)
                    for t in range(2):
                        tile = base[:, bass.ds(2 * u + t, 1), :].rearrange("p a c -> p (a c)")
                        last = nc.vector.scalar_tensor_tensor(
                            tile, yv[par][:, 2 * t + k, :],
                            gate[:, k, bass.ds(2 * u + t, 1)],
                            tile, ALU.mult, ALU.add)
                    last.then_inc(s_cmid if k == 0 else s_comb, 1)
                return [lambda: add(0), lambda: add(1)]

            def units(a, b):
                return [f for u in range(a, b) for f in unit_steps(u)]

            def split(g, half):
                dve.wait_ge(s_xhi, g + 1)
                nc.vector.tensor_tensor(x_lo[:, :, :], (x1 if half == 0 else x_re)[:, :, :],
                                        x_hi[:, :, :].bitcast(F32), ALU.subtract).then_inc(s_xlo, 1)

            def split_first():
                for c in range(CC):
                    if c < CC - 1:
                        dve.wait_ge(s_part, 2 * c + 1)
                    else:
                        dve.wait_ge(s_xhi, 1)
                    nc.vector.tensor_tensor(x_lo[:, c, :], x1[:, c, :], x_hi[:, c, :].bitcast(F32),
                                            ALU.subtract).then_inc(s_xlo if c == CC - 1 else s_part, 1)

            def finish(g, units_added=0):
                after(dve, s_comb, units_added)
                dve.wait_ge(s_down, (g + 1) * SB)
                rows_stored(dve, g // HG, g)
                for d in range(2):
                    rows = base[:, bass.ds(g * TT + 2 * d, 2), :].rearrange("p t c -> p (t c)")
                    nc.vector.scalar_tensor_tensor(rows, ps_d[d][:, :], THIRD, rows,
                                                   ALU.mult, ALU.add).then_inc(s_base, 1)

            def shared(g, fill, ahead, half, behind=None, units_added=0):
                for f in fill[0]:
                    f()
                if behind is not None:
                    finish(behind, units_added)
                for b in range(SB):
                    dve.wait_ge(s_act, g * SB + b + 1)
                    after(dve, s_hhi, g * SB + b - 1)
                    after(dve, s_hlo, g * SB + b - 1)
                    if g in (HG, HG + 1) and b < 2:
                        dve.wait_ge(s_yst[b], 16 * (g - HG + 1) * STEPS // 2)
                    nc.vector.tensor_tensor(hid[:, b % 2, :], act[:, b % 2, :], ps[2 * (b % 2) + 1][:, :],
                                            ALU.mult).then_inc(s_hid, 1)
                    early = 2 if (g, b) == (HG - 1, 0) else 1 if g < HG - 1 and (g, b) != (0, 0) else 0
                    for f in fill[b + 1][0:early]:
                        f()
                    dve.wait_ge(s_hhi, g * SB + b + 1)
                    after(dve, s_down, g * SB + b + 1 - SB)
                    if g in (HG, HG + 1) and b < 2:
                        dve.wait_ge(s_edn, (g - HG + 1) * STEPS - 1 + b)
                    nc.vector.tensor_tensor(hid_lo[:, b, :], hid[:, b % 2, :], hid_hi[:, b, :].bitcast(F32),
                                            ALU.subtract).then_inc(s_hlo, 1)
                    if b == SB - 1 and ahead is not None:
                        split(ahead, half)
                    for f in fill[b + 1][early:]:
                        f()

            def spread(steps, shares):
                lists, at = [], 0
                for n in shares:
                    lists.append(steps[at:at + n])
                    at += n
                assert at >= len(steps)
                return lists

            def experts(h):
                for s in range(STEPS + 3):
                    i = turn_of(h, s)
                    S = STEPS * h + s
                    if h == 0 and s == STEPS + 1:
                        split(HG, 1)
                    if s < STEPS:
                        dve.wait_ge(s_exhi, S + 1)
                        after(dve, s_eup, S - 1)
                        nc.vector.tensor_tensor(xt_lo[s % 2].rearrange("p c s -> p (c s)"), ps_x[s % 2][:, :],
                                                xt_hi[s % 2].rearrange("p c s -> p (c s)").bitcast(F32),
                                                ALU.subtract).then_inc(s_exlo, 1)
                    if 2 <= s <= STEPS + 1:
                        dve.wait_ge(s_ehhi, S - 1)
                        after(dve, s_edn, S - 3)
                        nc.vector.tensor_tensor(ht_lo[s % 2].rearrange("p c s -> p (c s)"), ps_h[s % 2][:, :],
                                                ht_hi[s % 2].rearrange("p c s -> p (c s)").bitcast(F32),
                                                ALU.subtract).then_inc(s_ehlo, 1)
                    n = (0, 5, 8, 14, FRONT_STEPS)
                    if i is not None and s % XR == 0:
                        for f in front_steps(HG + i)[n[3]:]:
                            f()
                    if h == 0 and s % XR and front_beside(s) is not None:
                        for f in front_steps(front_beside(s))[n[s % XR - 1]:n[s % XR]]:
                            f()
                    if i == TURNS - 1 and s % XR >= 2:
                        place[1][s % XR - 2]()
                    if h == 0 and s in (STEPS, STEPS + 2):
                        place[1][2 + (s - STEPS) // 2]()
                    if h == 1 and (s < 2 or unit_beside(s - 2) is not None):
                        for f in unit_steps(s if s < 2 else unit_beside(s - 2)):
                            f()

            dve.wait_ge(s_const, 9)
            fronts = [f for g in range(HG) for f in front_steps(g)]
            lead = FRONT_STEPS + FRONT_STEPS // CC - 1
            for f in fronts[0:FRONT_STEPS]:
                f()
            split_first()
            dve.wait_ge(s_small, 16 * 3)
            for c in range(CC):
                nc.vector.tensor_tensor(cond_rw[:, c, :, :], cond[:, c, :].unsqueeze(2).to_broadcast([P, NB, E]),
                                        rw[:, CC + c, :].unsqueeze(1).to_broadcast([P, NB, E]),
                                        ALU.mult).then_inc(s_crw, 1)
            for f in fronts[FRONT_STEPS:lead]:
                f()
            for g in range(HG - 1):
                todo = fronts[lead + g * FRONT_STEPS:lead + (g + 1) * FRONT_STEPS]
                shared(g, spread(todo, (6, 4, 5, 3, 0) if g > 0 else (0, 6, 9, 3, 0)), g + 1, 0, g - 1 if g > 0 else None)
            dve.wait_ge(s_clc, 1)
            place = [place_steps(h) for h in range(HALVES)]
            p = place[0]
            shared(HG - 1, [[p[0], p[1], p[2]], [lambda: finish(HG - 2), p[3]], p[4:10], p[10:11], p[11:]], None, 0)
            finish(HG - 1)
            experts(0)
            p = place[1]
            for f in p[4:7]:
                f()
            shared(HG, [[], p[7:9], p[9:11], p[11:], []], HG + 1, 1)
            finish(HG)
            experts(1)
            shared(HG + 1, [[], [], [], [], units(8, 10)], HG + 2, 1)
            shared(HG + 2, [[], [], units(10, 11), units(11, 12), unit_steps(12, True)], HG + 3, 1, HG + 1)
            shared(HG + 3, [[], units(13, 14), unit_steps(14, True), [], unit_steps(15, True)], None, 1, HG + 2, 13)
            finish(HG + 3, UNITS)

        @block.tensor
        def _(pe):
            def three(out, x_hi, x_lo, w_hi, w_lo, start, stop):
                nc.tensor.matmul(out, x_hi, w_hi, start=start, stop=False, skip_group_check=True)
                nc.tensor.matmul(out, x_lo, w_hi, start=False, stop=False, skip_group_check=True)
                return nc.tensor.matmul(out, x_hi, w_lo, start=False, stop=stop, skip_group_check=True)

            def up(g, b, between=None):
                after(pe, s_hid, g * SB + b - 1)
                for half in range(2):
                    if half == 1 and between is not None:
                        between()
                    for c in range(CC):
                        col = UP_S + ((b * 2 + half) * CC + c) * P
                        wh, wl = w_hi[:, col:col + P], w_lo[:, col:col + P]
                        last = three(ps[2 * (b % 2) + half][:, :], wh, wl, x_hi[:, c, :], x_lo[:, c, :],
                                     c == 0, c == CC - 1)
                last.then_inc(s_up, 1)

            def down(g, b):
                pe.wait_ge(s_hhi, g * SB + b + 1)
                pe.wait_ge(s_hlo, g * SB + b + 1)
                if b == 0:
                    after(pe, s_base, 2 * g)
                col = DN_S + b * C
                for t in range(TT):
                    toks = slice(t * P, (t + 1) * P)
                    last = three(ps_d[t // 2][:, (t % 2) * C:(t % 2 + 1) * C], hid_hi[:, b, toks], hid_lo[:, b, toks],
                                 w_hi[:, col:col + C], w_lo[:, col:col + C], b == 0 and t % 2 == 0, b == SB - 1)
                last.then_inc(s_down, 1)

            def logits(g, n):
                pe.wait_ge(s_front, (g + 1) * FRONT_STEPS)
                for t in range(TT):
                    for c in range(CC):
                        last = nc.tensor.matmul(ps_r[:, bass.ds(n * TT * E + t * E, E)], x1[:, c, t * P:(t + 1) * P],
                                                rw[:, c, :], start=(c == 0), stop=(c == CC - 1))
                last.then_inc(s_logit, 1)

            def to_rows(g, r):
                after(pe, s_xev, 2 * g + r)
                for t in range(2):
                    for c in range(CC):
                        n = (2 * r + t) * P
                        last = nc.tensor.transpose(ps_t[:, t * C + c * P:t * C + (c + 1) * P], x1[:, c, n:n + P],
                                                   ident[:, :])
                last.then_inc(s_xt, 1)

            def ranks(h):
                pe.wait_ge(s_place, h * PLACE_STEPS + PREFIX_STEP)
                dst = ps_r[:, HT * E:2 * HT * E]
                nc.tensor.matmul(dst, earlier[:, :], member[:, :, :].rearrange("p e t -> p (e t)"), start=True, stop=False)
                nc.tensor.matmul(dst, ones[:, 0:P], prefix_x[:, :, :].rearrange("p e t -> p (e t)"), start=False, stop=True)
                nc.tensor.matmul(ps_r[:, 2 * HT * E:2 * HT * E + E], ones[:, 0:P], prefix[:, :, HT - 1],
                                 start=True, stop=True).then_inc(s_ranks, 1)

            def slot_tokens(h, a, b):
                pe.wait_ge(s_xev, 2 * HG * (h + 1))
                pe.wait_ge(s_place, h * PLACE_STEPS + TILE_STEP)
                for n in range(a, b):
                    pe.wait_ge(s_hot, h * BATCHES + n + 1)
                    if n == BATCHES // 2:
                        pe.wait_ge(s_thot, h + 1)
                    for j in range(n * HOTS, (n + 1) * HOTS):
                        last = nc.tensor.matmul(ps_t[:, 0:TILES], lane_hot[:, n % 2, j % HOTS, :], tile_hot[:, j, :],
                                                start=(j == 0), stop=(j == INST - 1))
                    last.then_inc(s_used, 1)

            def cond_products():
                pe.wait_ge(s_small, 16 * 3)
                pe.wait_ge(s_crw, CC)
                for c in range(CC):
                    last = nc.tensor.matmul(ps_r[:, PS_COND:PS_COND + NB * E], ones[:, 0:P],
                                            cond_rw[:, c, :, :].rearrange("p b e -> p (b e)"),
                                            start=(c == 0), stop=(c == CC - 1))
                last.then_inc(s_cl, 1)
                pe.wait_ge(s_clc, 1)

            def shared(g, ahead=None, h=None):
                pe.wait_ge(s_xlo, g + 1)
                if g == 0:
                    pe.wait_ge(s_part, 2)
                    pe.wait_ge(s_wlo, 1)
                if g not in (HG, HG + 1):
                    up(g, 0)
                if g == HG - 1:
                    to_rows(g, 1)
                up(g, 1, (lambda: ranks(0)) if h == 0 else None)
                if g == 0:
                    to_rows(0, 1)
                    cond_products()
                    logits(0, 0)
                    pe.wait_ge(s_wlo, 2)
                if h == 1:
                    slot_tokens(1, 0, BATCHES // 2)
                up(g, 2)
                if h == 1:
                    slot_tokens(1, BATCHES // 2, BATCHES)
                if g == 0:
                    pe.wait_ge(s_wlo, SHARED_CHUNKS)
                down(g, 0)
                up(g, 3)
                down(g, 1)
                if h == 0:
                    slot_tokens(0, 0, BATCHES)
                down(g, 2)
                if ahead is not None:
                    logits(ahead, ahead)
                    to_rows(ahead, 0)
                down(g, 3)
                if ahead is not None and ahead < HG - 1:
                    to_rows(ahead, 1)

            def experts(h):
                weights_of = {}

                def to_channels(S, s):
                    pe.wait_ge(s_xg[s % XR], 2 * 16 * (STEPS // XR * h + s // XR + 1))
                    after(pe, s_exlo, S - 1)
                    for u in range(2):
                        for c in range(CC):
                            last = nc.tensor.transpose(ps_x[s % 2][:, c * 2 * P + u * P:c * 2 * P + (u + 1) * P],
                                                       xg[:, s % XR, u, c * P:(c + 1) * P], ident[:, :])
                    last.then_inc(s_ext, 1)

                def load_experts(s):
                    _, loaded = nc.values_load_multi_w_load_instructions(
                        exp_i[h][0:1, 2 * s:2 * s + 4], engines=[mybir.EngineType.PE],
                        min_val=0, max_val=(E - 1) * CHUNK)
                    for n in range(4):
                        weights_of[2 * s + n] = loaded[n]
                        weights_of.pop(2 * (s - 5) + n, None)

                def products(bank, hi, lo, s, first):
                    for u in range(2):
                        e = weights_of[2 * s + u]
                        for c in range(CC):
                            col = e + (EXP + first + c * C)
                            last = three(bank[:, u * C:(u + 1) * C], hi[:, c, u * P:(u + 1) * P],
                                         lo[:, c, u * P:(u + 1) * P], w_hi[:, bass.ds(col, C)],
                                         w_lo[:, bass.ds(col, C)], c == 0, c == CC - 1)
                    return last

                pe.wait_ge(s_place, h * PLACE_STEPS + EXPERT_STEP)
                load_experts(0)
                pe.wait_ge(s_wlo, NCHUNK)
                pe.wait_ge(s_hid, (HG + h) * SB)
                for s in range(STEPS + 3):
                    i = turn_of(h, s)
                    S = STEPS * h + s
                    if s % 2 == 0 and 0 < s < STEPS:
                        load_experts(s)
                    if s == 1:
                        pe.wait_ge(s_base, 2 * (HG + h))
                    if s < STEPS:
                        to_channels(S, s)
                    if i is not None and s % XR == 2:
                        if i < TURNS - 1:
                            logits(HG + i, i)
                        to_rows(HG + i, 0)
                    if 1 <= s <= STEPS:
                        pe.wait_ge(s_exlo, S)
                        after(pe, s_ege, S - 1)
                        products(ps[1], xt_hi[(s - 1) % 2], xt_lo[(s - 1) % 2], s - 1, 0).then_inc(s_eup, 1)
                    if 2 <= s <= STEPS + 1:
                        pe.wait_ge(s_ege, S - 1)
                        after(pe, s_ehlo, S - 3)
                        for u in range(2):
                            for m in range(CC):
                                last = nc.tensor.transpose(ps_h[s % 2][:, m * 2 * P + u * P:m * 2 * P + (u + 1) * P],
                                                           gelu[:, s % 2, u * C + m * P:u * C + (m + 1) * P],
                                                           ident[:, :])
                        last.then_inc(s_eht, 1)
                    if s == STEPS + 2:
                        pe.wait_ge(s_xlo, HG + h + 1)
                        pe.wait_ge(s_ege, STEPS * (h + 1))
                        up(HG + h, 0)
                    if 3 <= s:
                        pe.wait_ge(s_ehlo, S - 2)
                        after(pe, s_ey, S - 3)
                        products(ps[3], ht_hi[(s - 3) % 2], ht_lo[(s - 3) % 2], s - 3, CC * C).then_inc(s_edn, 1)
                    if i == TURNS - 1 and s % XR == 1:
                        logits(HG + i, i)
                    if i is not None and s % XR == 2:
                        to_rows(HG + i, 1)
                    if h == 0 and s == STEPS + 1:
                        ranks(1)


            pe.wait_ge(s_const, 9)
            pe.wait_ge(s_front, FRONT_STEPS)
            to_rows(0, 0)
            for g in range(HG - 1):
                shared(g, g + 1)
            shared(HG - 1, None, 0)
            experts(0)
            pe.wait_ge(s_ey, STEPS)
            shared(HG, None, 1)
            experts(1)
            pe.wait_ge(s_ey, 2 * STEPS)
            for g in range(HG + 1, NG):
                shared(g)


def kernel(**inputs):
    import numpy as np
    import concourse.bacc as bacc
    from concourse.bass_utils import run_bass_kernel_spmd

    f = {k: np.asarray(v) for k, v in inputs.items()}
    x = f["x"]
    B, seq, C = x.shape
    CC = C // P
    N = B * seq
    w1, w3, w2 = f["L1_cond_w1"], f["L1_cond_w3"], f["L1_cond_w2"]
    w1e, w2e = f["L1_cond_W1e"], f["L1_cond_W2e"]
    E = w1e.shape[0]

    cols = []
    for b in range(w1.shape[1] // P):
        for w in (w1, w3):
            for c in range(CC):
                cols.append(w[c * P:(c + 1) * P, b * P:(b + 1) * P])
    for b in range(w2.shape[0] // P):
        cols.append(w2[b * P:(b + 1) * P, :])
    for e in range(E):
        for w in (w1e[e], w2e[e]):
            for c in range(CC):
                cols.append(w[c * P:(c + 1) * P, :])
    arrays = {
        "x_t": np.ascontiguousarray(x.transpose(2, 0, 1).reshape(CC, P, N)),
        "cond_t": np.ascontiguousarray(f["cond_1024"].T.reshape(CC, P, B).transpose(1, 0, 2)),
        "router_w": np.ascontiguousarray(f["L1_cond_router_W"].reshape(2 * CC, P, E).transpose(1, 0, 2)),
        "router_b": np.ascontiguousarray(f["L1_cond_router_bias"]),
        "w_all": np.ascontiguousarray(np.concatenate(cols, axis=1)),
    }
    nc = bacc.Bacc("TRN2", target_bir_lowering=False, num_devices=1)
    F32 = mybir.dt.float32
    aps = [nc.dram_tensor(n, a.shape, mybir.dt.from_np(a.dtype), kind="ExternalInput").ap() for n, a in arrays.items()]
    out = nc.dram_tensor("out", (N, C), F32, kind="ExternalOutput").ap()
    x1_cols = nc.dram_tensor("x1_cols", (N // GT // HALVES, P, CC * GT), F32, kind="Internal").ap()
    x1_rows = [nc.dram_tensor(f"x1_rows{h}", (N // HALVES, C), F32, kind="Internal").ap() for h in range(HALVES)]
    slots = expert_tiles(N // HALVES, E) * P
    y_rows = [nc.dram_tensor(f"y_rows{h}", (slots, C), F32, kind="Internal").ap() for h in range(HALVES)]
    build_spiking_moe(nc, *aps, out, x1_cols, x1_rows, y_rows)
    r = run_bass_kernel_spmd(nc, [arrays], core_ids=[0])
    return r.results[0]["out"].reshape(B, seq, C)
```
